# Optimizing a Trainium2 kernel written in Bass

```python
import numpy as np
import jax
import jax.numpy as jnp

def _softmax(x, axis=-1):
    return jax.nn.softmax(x, axis=axis)

def _gelu(x):
    return jax.nn.gelu(x, approximate=True)

def _silu(x):
    return jax.nn.silu(x)

def _sigmoid(x):
    return jax.nn.sigmoid(x)

def _layernorm(x, axis=-1, eps=1e-05):
    m = jnp.mean(x, axis=axis, keepdims=True)
    v = jnp.var(x, axis=axis, keepdims=True)
    return (x - m) / jnp.sqrt(v + eps)

def _scatter_add(tgt, idx, src, axis=0):
    return tgt.at[idx].add(src)

def _segment_sum(src, seg, n):
    return jax.ops.segment_sum(src, seg, n)
kernel_name = 'mk_adj_resnorm_d1_adj_r2_b8f45a'

def setup_inputs(seed: int=0):
    np.random.seed(seed)
    _w = jnp.asarray

    def _rec_inputs():
        import jax
        import jax.numpy as jnp
        _gk = jax.random.key(seed)
        x = -0.0005146 + 1 * jax.random.normal(jax.random.fold_in(_gk, 1), (8, 1024, 128), jnp.float32)
        _w = (1.0 + jnp.arange(1024, dtype=jnp.float32)) ** (-0.5)
        _w = _w / _w.mean()
        _pij = jnp.clip(0.00390625 * _w[:, None] * _w[None, :], 0.0, 1.0)
        _a = jax.random.uniform(jax.random.fold_in(_gk, 2), (8, 1024, 1024)) < _pij
        adj = _a.astype(jnp.int32)
        return (x, adj)
    x, adj = _rec_inputs()

    def _L0_gnn_setup():
        import jax, jax.numpy as jnp
        import numpy as np
        B, N, C, OUT, S = (4, 1024, 128, 128, 25)
        DENSITY = 0.008
        key = jax.random.key(seed)
        kA, kX, kW = jax.random.split(key, 3)
        A = jax.random.bernoulli(kA, DENSITY, (B, N, N)).astype(jnp.int32)
        X = jax.random.normal(kX, (B, N, C), dtype=jnp.float32)
        W = jax.random.normal(kW, (2 * C, OUT), dtype=jnp.float32) * np.float32(1.0 / np.sqrt(2 * C))
        b = jnp.zeros((OUT,), dtype=jnp.float32)
        return {'A': A, 'X': X, 'W': W, 'b': b}
    _L0_gnn_all = _L0_gnn_setup()
    _L0_gnn_in = {k: v for k, v in _L0_gnn_all.items() if k in ('W', 'b')}
    del _L0_gnn_all
    return {'x': x, 'adj': adj, 'L0_gnn_W': _L0_gnn_in['W'], 'L0_gnn_b': _L0_gnn_in['b']}

def reference(x, adj, L0_gnn_W, L0_gnn_b):
    import jax
    import jax.numpy as jnp

    def _L0_gnn_ref(A, X, W, b):
        import jax, jax.numpy as jnp
        import numpy as np
        B, N, C, OUT, S = (4, 1024, 128, 128, 25)
        DENSITY = 0.008
        mask = A != 0
        neg_inf = jnp.float32(-jnp.inf)
        pri = -jnp.arange(N, dtype=jnp.float32)
        scores = jnp.where(mask, pri, neg_inf)
        vals, idx = jax.lax.top_k(scores, S)
        valid = vals > neg_inf
        feats = jax.vmap(lambda x, i: x[i])(X, idx)
        feats = jnp.where(valid[..., None], feats, neg_inf)
        agg = feats.max(axis=2)
        degree = mask.sum(axis=-1)
        agg = jnp.where((degree <= S)[..., None], jnp.maximum(agg, 0.0), agg)
        h = jnp.concatenate([X, agg], axis=-1)
        out = jax.nn.relu(jnp.einsum('bnf,fo->bno', h, W) + b)
        return out
    x = _layernorm(x + _L0_gnn_ref(adj, x, L0_gnn_W, L0_gnn_b), axis=-1)
    return x

_drawn_inputs = setup_inputs


def setup_inputs(seed=0):
    import zlib

    import numpy as np

    out = dict(_drawn_inputs(seed))
    spreads = {'L0_gnn_b': (0.0, 0.1)}
    factors = {}
    for name, (base, spread) in spreads.items():
        noise = np.random.default_rng([zlib.crc32(name.encode()), seed]).standard_normal(out[name].shape)
        drawn = base * np.exp(spread * noise) if base else spread * noise
        out[name] = jnp.asarray(drawn.astype(out[name].dtype))
    for name, factor in factors.items():
        out[name] = (out[name] * factor).astype(out[name].dtype)
    return out
```

```python
from contextlib import ExitStack

import numpy as np

import concourse.bass as bass
from concourse import mybir

ALU = mybir.AluOpType
ACT = mybir.ActivationFunctionType
AX = mybir.AxisListType
F32 = mybir.dt.float32
F16 = mybir.dt.float16
BF16 = mybir.dt.bfloat16
I32 = mybir.dt.int32
U32 = mybir.dt.uint32

P = 128
B, N, C = 8, 1024, 128
S = 25
T = N // P
EPS = 1e-5
BIG = 3.0e38

BITS = 8
G = N // BITS
GB = P // BITS
PK = GB + 1
CLS = S + 2
TABLE = N + 1

FULL = 10
HALF = 4
QUARTER = S - FULL - HALF
N_HALF, N_QUARTER = HALF // 2, -(-QUARTER // 4)
SLOTS = [FULL + N_HALF + N_QUARTER, 7, 5, 4, 3, 3, 2, 1]
FIRST = [sum(SLOTS[:t]) for t in range(T + 1)]
LIMIT = [2.0 * N] * CLS
LIMIT[FULL], LIMIT[FULL + HALF] = P // 2, P // 4
for _t in range(T - 1, 0, -1):
    LIMIT[SLOTS[_t]] = min(LIMIT[SLOTS[_t]], _t * P)

V0 = 32
V1 = 8
NV = V0 + (T - 1) * V1
SCALAR_TILES = 4
SPARE = 5
NF = N_HALF + N_QUARTER
FOLD = NV

CONST = {}
_at = 0
for _name, _w in (("pack", PK), ("before", P), ("ident", P), ("base", G), ("classes", CLS),
                  ("limit", CLS), ("bit", BITS), ("power", BITS), ("offset", B), ("node", T), ("minus_node", T), ("count", N)):
    CONST[_name] = (_at, _at + _w)
    _at += _w
NCONST = _at


def constants():
    c = np.zeros((P, NCONST), np.float32)
    p = np.arange(P)

    def put(name, a):
        c[:, CONST[name][0]:CONST[name][1]] = a

    pack = np.zeros((P, PK), np.float32)
    pack[p, p // BITS] = 2.0 ** (p % BITS)
    pack[:, GB] = 1.0
    put("pack", pack)
    put("before", p[:, None] < p[None, :])
    put("ident", p[:, None] == p[None, :])
    put("base", (G - np.arange(G)) * 2.0 ** BITS)
    put("classes", np.arange(CLS))
    put("limit", np.array(LIMIT))
    put("bit", np.arange(BITS))
    put("power", 2.0 ** np.arange(BITS))
    put("offset", np.arange(B) * TABLE)
    put("node", p[:, None] + P * np.arange(T)[None, :])
    put("minus_node", -(p[:, None] + P * np.arange(T)[None, :]))
    put("count", np.arange(N))
    return c


def gnn_kernel(nc, x, x_t, table, adj_t, w, bias, const, out):
    with ExitStack() as ctx:
        def sb(name, shape, dt):
            return ctx.enter_context(nc.sbuf_tensor(name, shape, dt))

        def bank(name):
            return ctx.enter_context(nc.psum_tensor(name, [P, 512], F32))

        def sem(name):
            return ctx.enter_context(nc.semaphore(name))

        cst = sb("cst", [P, NCONST], F32)
        pack = sb("pack", [P, PK], BF16)
        before = sb("before", [P, P], BF16)
        ident = sb("ident", [P, P], F16)
        base = sb("base", [P, G], BF16)
        count = sb("count", [P, N], F16)
        power = sb("power", [P, BITS], I32)
        ones = sb("ones", [P, P], BF16)
        ones_row = sb("ones_row", [1, P], F32)
        eps = sb("eps", [P, 1], F32)
        w_self = sb("w_self", [P, C], F32)
        w_agg = sb("w_agg", [P, C], F32)
        bias_row = sb("bias_row", [1, C], F32)

        raw = sb("raw", [P, T, N], I32)
        mask = sb("mask", [P, T, N], BF16)
        bits = sb("bits", [P, T, T, PK], BF16)
        high = sb("high", [P, T, G], BF16)
        degree = sb("degree", [P, T], F32)
        cls = sb("cls", [P, T], F32)
        same = sb("same", [P, T, CLS], BF16)
        above = sb("above", [P, T, CLS], BF16)
        picked = sb("picked", [P, T, CLS], F32)
        rank = sb("rank", [P, T], F32)
        rank16 = sb("rank16", [P, T], F16)
        rank_row = sb("rank_row", [P, 2, N], F16)
        distance = sb("distance", [P, 2, N], F16)
        n_above = sb("n_above", [P, CLS], F32)
        broken = sb("broken", [P, CLS], F32)
        n_broken = sb("n_broken", [P, 1], F32)
        spare_flag = sb("spare_flag", [P, B], I32)
        floor = sb("floor", [P, B, T], F32)
        perm = sb("perm", [P, T, N], BF16)
        perm_t = sb("perm_t", [P, 2, T, N], BF16)
        keys = sb("keys", [P, T, G], F32)
        keys_left = sb("keys_left", [P, G], F32)
        tops = sb("tops", [P, NV], F32)
        tops_i = sb("tops_i", [P, NV], I32)
        tops_8 = sb("tops_8", [P, NV], I32)
        numbered = sb("numbered", [P, NV, BITS], F32)
        set_bits = sb("set_bits", [P, NV, BITS], I32)
        found = sb("found", [P, NV, BITS], F32)
        near = sb("near", [P, NV + NF], F32)
        index = sb("index", [P, 2, NV + NF], U32)
        rows = sb("rows", [P, FIRST[T], C], F32)
        head = sb("head", [P, 7, C], F32)
        agg = sb("agg", [P, T, C], F32)
        rest = sb("rest", [P, T, C], F32)
        part = sb("part", [P, 3, T, C], BF16)
        agg_t = sb("agg_t", [P, N], F32)
        x_in = sb("x_in", [P, T, C], F32)
        xt_in = sb("xt_in", [P, N], F32)
        z = sb("z", [P, T, C], F32)
        stats = sb("stats", [P, T, 6], F32)
        mean_var = sb("mean_var", [P, T, 2], F32)
        std = sb("std", [P, T], F32)
        inv_std = sb("inv_std", [P, T], F32)
        shift = sb("shift", [P, T], F32)
        y = sb("y", [P, T, C], F32)
        sp_keys = sb("sp_keys", [P, G], F32)
        sp_index = sb("sp_index", [P, V0], U32)
        sp_rows = sb("sp_rows", [P, SPARE, C], F32)
        sp_agg = sb("sp_agg", [P, 2, T, C], F32)

        banks = [bank(f"bank{i}") for i in range(8)]
        PER = [3, 3, 2]

        def bits_ps(i):
            return banks[i][:, 0:PER[i] * T * PK].rearrange("p (t j k) -> p t j k", t=PER[i], k=PK)

        rank_ps = banks[3][:, 0:T * CLS].rearrange("p (t d) -> p t d", t=T)
        above_ps = banks[3][:, T * CLS:(T + 1) * CLS]
        aggt_ps, out_ps = banks[6], banks[7]

        s_const = sem("constants_loaded")
        s_ready = sem("constants_made")
        s_raw = [sem(f"raw_loaded_{q}") for q in range(4)]
        s_mask = sem("mask_made")
        s_packed = sem("bits_packed")
        s_bits = sem("bits_copied")
        s_high = sem("high_made")
        s_class = sem("classes_made")
        s_ranked = sem("rank_sums_made")
        s_rank = sem("rank_made")
        s_above = sem("above_kept")
        s_row_ps = sem("rank_row_made")
        s_row = sem("rank_row_copied")
        s_perm = sem("perm_made")
        s_sorted = sem("keys_sorted")
        s_keys = sem("keys_copied")
        s_extract = sem("keys_used")
        s_index = sem("index_made")
        s_rows = [sem(f"rows_gathered_{t}") for t in range(T)]
        s_reduced = sem("rows_reduced")
        s_free = [sem(f"rows_free_{t}") for t in range(T)]
        s_agg = sem("agg_made")
        s_hi = sem("hi_made")
        s_rest = sem("rest_made")
        s_mid = sem("mid_made")
        s_lo = sem("lo_made")
        s_permt = sem("perm_t_made_by_vector")
        s_permt_a = sem("perm_t_made_by_scalar")
        s_distance = sem("distance_made")
        s_turned = sem("agg_turned")
        s_aggt = sem("agg_t_copied")
        s_x = sem("x_loaded")
        s_lin = sem("linear_made")
        s_z = sem("z_made")
        s_var = sem("variance_made")
        s_std = sem("std_made")
        s_inv = sem("inverse_std_made")
        s_y = sem("y_made")
        s_out = [sem(f"out_stored_{h}") for h in range(2)]
        s_spidx = sem("spare_index_made")
        s_sprows = sem("spare_rows_gathered")
        s_spfree = sem("spare_rows_free")
        s_step = sem("vector_steps")

        def wait(eng, s, value):
            if not isinstance(value, int) or value > 0:
                eng.wait_ge(s, value)

        block = ctx.enter_context(nc.Block())


        @block.sync
        def _(sp):
            sp.dma_start(cst[:, :], const).then_inc(s_const, 16)
            sp.dma_start(w_self[:, :], w[0:C, :]).then_inc(s_const, 16)
            sp.dma_start(w_agg[:, :], w[C:2 * C, :]).then_inc(s_const, 16)
            sp.dma_start(bias_row[:, :], bias).then_inc(s_const, 16)

            def load_adj(n):
                for q in range(4):
                    wait(sp, s_mask, 4 * (n - 1) + q + 1)
                    sp.dma_start(raw[:, 2 * q:2 * q + 2, :],
                                 adj_t[bass.ds(n, 1), 2 * q * P:(2 * q + 2) * P, :]
                                 .rearrange("a (j p) i -> p (a j) i", p=P)).then_inc(s_raw[q], 16)

            def load_x(n):
                wait(sp, s_z, 2 * n)
                wait(sp, s_lin, 2 * n)
                sp.dma_start(x_in[:, :, :], x[bass.ds(n, 1), :, :].rearrange("a (t p) c -> p (a t) c", p=P)).then_inc(s_x, 16)
                sp.dma_start(xt_in[:, :], x_t[bass.ds(n, 1), :, :].rearrange("a c i -> c (a i)")).then_inc(s_x, 16)

            load_adj(0)
            load_adj(1)
            load_adj(2)
            load_x(0)
            with sp.Fori(1, B - 2) as n:
                load_adj(n + 2)
                load_x(n)
            load_x(B - 2)
            load_x(B - 1)

        @block.gpsimd
        def _(pool):
            def gather(dst, idx, done):
                pool.indirect_dma_start(dst, None, table, bass.IndirectOffsetOnAxis(ap=idx, axis=0)).then_inc(done, 16)

            def spare(n):
                flag = pool.value_load(spare_flag[0:1, bass.ds(n, 1)], min_val=0, max_val=CLS)
                with pool.If(flag > 0):
                    with pool.Fori(0, T):
                        pool.wait_ge(s_spidx, 1)
                        pool.sem_clear(s_spidx)
                        for k in range(S):
                            if k % SPARE == 0 and k > 0:
                                pool.wait_ge(s_spfree, 1)
                                pool.sem_clear(s_spfree)
                            gather(sp_rows[:, k % SPARE, :], sp_index[:, k:k + 1], s_sprows)

            def gathers(n, side):
                pool.wait_ge(s_index, n + 1)
                spare(n)
                for t in range(T):
                    if not isinstance(n, int) or n > 0:
                        pool.wait_ge(s_free[t], 1)
                        pool.sem_clear(s_free[t])
                    columns = (list(range(FULL)) + list(range(FOLD, FOLD + NF)) if t == 0 else
                               [V0 + V1 * (t - 1) + k for k in range(SLOTS[t])])
                    for k, col in enumerate(columns):
                        gather(rows[:, FIRST[t] + k, :], index[:, side, col:col + 1], s_rows[t])

            gathers(0, 0)
            gathers(1, 1)
            with pool.Fori(1, B // 2) as pair:
                gathers(2 * pair, 0)
                gathers(2 * pair + 1, 1)

        @block.tensor
        def _(pe):
            def pack_bits(n):
                if isinstance(n, int) and n == 0:
                    pe.wait_ge(s_ready, 1)
                wait(pe, s_row, n)
                wait(pe, s_class, n)
                wait(pe, s_bits, 3 * n)
                for j in range(T):
                    if j % 2 == 0:
                        pe.wait_ge(s_mask, 4 * n + j // 2 + 1)
                    for t in range(T):
                        last = nc.tensor.matmul(bits_ps(t // 3)[:, t % 3, j, :], mask[:, j, t * P:(t + 1) * P],
                                                pack[:, :], start=True, stop=True)
                last.then_inc(s_packed, 1)

            def rank_nodes(n):
                pe.wait_ge(s_class, n + 1)
                wait(pe, s_above, n)
                wait(pe, s_rank, n)
                nc.tensor.matmul(rank_ps[:, :, :], before[:, :], same[:, :, :], start=True, stop=False)
                for t in range(T - 1):
                    nc.tensor.matmul(rank_ps[:, t + 1:, :], ones[:, :],
                                     same[:, t:t + 1, :].to_broadcast([P, T - 1 - t, CLS]), start=False, stop=False)
                for t in range(T):
                    nc.tensor.matmul(rank_ps[:, :, :], ones[:, :], above[:, t:t + 1, :].to_broadcast([P, T, CLS]),
                                     start=False, stop=(t == T - 1))
                for t in range(T):
                    last = nc.tensor.matmul(above_ps, ones[:, :], above[:, t, :], start=(t == 0), stop=(t == T - 1))
                last.then_inc(s_ranked, 1)

            def spread_rank(n):
                pe.wait_ge(s_rank, n + 1)
                pe.wait_ge(s_bits, 3 * (n + 1))
                for t in range(T):
                    last = nc.tensor.matmul(banks[t // 4][:, (t % 4) * P:(t % 4 + 1) * P],
                                            rank16[:, t:t + 1].to_broadcast([P, P]), ident[:, :], start=True, stop=True)
                last.then_inc(s_row_ps, 1)

            def sort_keys(n):
                wait(pe, s_keys, 2 * n)
                pe.wait_ge(s_high, n + 1)
                pe.wait_ge(s_perm, n + 1)
                for r in range(T):
                    dst = banks[4 + r // 4][:, (r % 4) * G:(r % 4 + 1) * G]
                    for t in range(T):
                        weights = perm[:, t, r * P:(r + 1) * P]
                        nc.tensor.matmul(dst, weights, bits[:, t, :, 0:GB], start=(t == 0), stop=False)
                        last = nc.tensor.matmul(dst, weights, high[:, t, :], start=False, stop=(t == T - 1))
                    if r % 4 == 3:
                        last.then_inc(s_sorted, 1)

            def turn_agg(n, side, h):
                if h == 0:
                    pe.wait_ge(s_permt, n + 1)
                    pe.wait_ge(s_permt_a, SCALAR_TILES * (n + 1))
                    pe.wait_ge(s_hi, n + 1)
                    pe.wait_ge(s_mid, n + 1)
                    pe.wait_ge(s_lo, n + 1)
                wait(pe, s_aggt, 2 * n + h)
                for r in range(T):
                    turned = perm_t[:, side, r, h * 512:(h + 1) * 512]
                    for k in range(3):
                        last = nc.tensor.matmul(aggt_ps[:, :], part[:, k, r, :], turned,
                                                start=(r == 0 and k == 0), stop=(r == T - 1 and k == 2))
                last.then_inc(s_turned, 1)

            def linear(n, h):
                pe.wait_ge(s_x, 32 * (n + 1))
                pe.wait_ge(s_aggt, 2 * n + h + 1)
                wait(pe, s_z, 2 * n + h)
                for t in range(4 * h, 4 * h + 4):
                    dst = out_ps[:, (t % 4) * C:(t % 4 + 1) * C]
                    nc.tensor.matmul(dst, ones_row[:, :], bias_row[:, :], start=True, stop=False)
                    nc.tensor.matmul(dst, xt_in[:, t * P:(t + 1) * P], w_self[:, :], start=False, stop=False)
                    last = nc.tensor.matmul(dst, agg_t[:, t * P:(t + 1) * P], w_agg[:, :], start=False, stop=True)
                last.then_inc(s_lin, 1)

            def sort(n):
                rank_nodes(n)
                spread_rank(n)
                sort_keys(n)

            def step(n, side, first=False, last=False):
                if not first:
                    turn_agg(n - 1, 1 - side, 0)
                if not last:
                    pack_bits(n + 2)
                if not first:
                    linear(n - 1, 0)
                    turn_agg(n - 1, 1 - side, 1)
                    linear(n - 1, 1)
                if not last:
                    sort(n + 2)

            for n in range(2):
                pack_bits(n)
                sort(n)
            step(0, 0, first=True)
            step(1, 1)
            with pe.Fori(1, B // 2 - 1) as pair:
                for side in range(2):
                    step(2 * pair + side, side)
            step(B - 2, 0, last=True)
            step(B - 1, 1, last=True)
            for h in range(2):
                turn_agg(B - 1, 1, h)
                linear(B - 1, h)

        @block.scalar
        def _(act):
            def copy_bits(n):
                act.wait_ge(s_packed, n + 1)
                wait(act, s_sorted, 2 * n)
                for i in range(3):
                    nc.scalar.copy(bits[:, 3 * i:3 * i + PER[i], :, :], bits_ps(i)).then_inc(s_bits, 1)

            def copy_ranks(n, side):
                act.wait_ge(s_row_ps, n + 1)
                wait(act, s_permt, n - 1)
                wait(act, s_permt_a, SCALAR_TILES * (n - 1))
                for h in range(2):
                    ins = nc.scalar.copy(rank_row[:, side, h * 512:(h + 1) * 512], banks[h][:, :])
                ins.then_inc(s_row, 1)

            def copy_keys(n):
                wait(act, s_extract, n)
                for h in range(2):
                    act.wait_ge(s_sorted, 2 * n + h + 1)
                    nc.scalar.copy(keys[:, 4 * h:4 * h + 4, :].rearrange("p t g -> p (t g)"),
                                   banks[4 + h][:, :]).then_inc(s_keys, 1)

            def split_agg(n):
                act.wait_ge(s_agg, n + 1)
                wait(act, s_turned, 2 * n)
                nc.scalar.copy(part[:, 0, :, :], agg[:, :, :]).then_inc(s_hi, 1)
                act.wait_ge(s_rest, n + 1)
                nc.scalar.copy(part[:, 1, :, :], rest[:, :, :]).then_inc(s_mid, 1)

            def transpose_perm(n, side, tiles):
                act.wait_ge(s_row, n + 1)
                wait(act, s_turned, 2 * (n - 1))
                for t in tiles:
                    wait(act, s_permt_a, SCALAR_TILES * n + t - 1)
                    nc.scalar.activation(distance[:, t % 2, :], rank_row[:, side, :],
                                         ACT.Abs, bias=cst[:, CONST["minus_node"][0] + t:CONST["minus_node"][0] + t + 1]
                                         ).then_inc(s_distance, 1)
                    act.wait_ge(s_distance, SCALAR_TILES * n + t + 1)
                    nc.scalar.activation(perm_t[:, side, t, :], distance[:, t % 2, :],
                                         ACT.Relu, bias=1.0, scale=-1.0).then_inc(s_permt_a, 1)

            def copy_turned(n, h):
                act.wait_ge(s_turned, 2 * n + h + 1)
                wait(act, s_lin, 2 * (n - 1) + h + 1)
                nc.scalar.copy(agg_t[:, h * 512:(h + 1) * 512], aggt_ps[:, :]).then_inc(s_aggt, 1)

            def root(n, h):
                act.wait_ge(s_var, 2 * n + h + 1)
                nc.scalar.activation(std[:, 4 * h:4 * h + 4], mean_var[:, 4 * h:4 * h + 4, 1], ACT.Sqrt,
                                     bias=eps[:, 0:1]).then_inc(s_std, 1)

            def normalise(n, h):
                act.wait_ge(s_inv, 2 * n + h + 1)
                wait(act, s_out[h], 16 * n)
                for t in range(4 * h, 4 * h + 4):
                    ins = nc.scalar.activation(y[:, t, :], z[:, t, :], ACT.Identity, bias=shift[:, t:t + 1],
                                               scale=inv_std[:, t:t + 1])
                ins.then_inc(s_y, 1)
                act.wait_ge(s_y, 2 * n + h + 1)
                act.dma_start(out[bass.ds(n, 1), h * 512:(h + 1) * 512, :].rearrange("a (t p) c -> p (a t) c", p=P),
                              y[:, 4 * h:4 * h + 4, :]).then_inc(s_out[h], 16)

            def step(n, side, first=False, last=False):
                half = SCALAR_TILES // 2
                transpose_perm(n, side, range(half))
                if not first:
                    copy_turned(n - 1, 0)
                transpose_perm(n, side, range(half, SCALAR_TILES))
                if not last:
                    copy_bits(n + 2)
                if not first:
                    root(n - 1, 0)
                    normalise(n - 1, 0)
                    copy_turned(n - 1, 1)
                    root(n - 1, 1)
                    normalise(n - 1, 1)
                if not last:
                    copy_ranks(n + 2, side)
                split_agg(n)
                if not last:
                    copy_keys(n + 2)

            act.wait_ge(s_ready, 1)
            for n in range(2):
                copy_bits(n)
                copy_ranks(n, n)
                copy_keys(n)
            step(0, 0, first=True)
            step(1, 1)
            with act.Fori(1, B // 2 - 1) as pair:
                for side in range(2):
                    step(2 * pair + side, side)
            step(B - 2, 0, last=True)
            step(B - 1, 1, last=True)
            for h in range(2):
                copy_turned(B - 1, h)
                root(B - 1, h)
                normalise(B - 1, h)
            for h in range(2):
                act.wait_ge(s_out[h], 16 * B)

        @block.vector
        def _(v):
            def const_of(name):
                return cst[:, CONST[name][0]:CONST[name][1]]

            class Steps:

                def __init__(self):
                    self.done = 0

                def __call__(self, ins):
                    ins.then_inc(s_step, 1)
                    self.done += 1

                def settle(self):
                    v.wait_ge(s_step, self.done)

                def end(self):
                    self.settle()
                    v.sem_clear(s_step)

            v.wait_ge(s_const, 64)
            setup = Steps()
            for dst, name in ((pack, "pack"), (before, "before"), (ident, "ident"), (base, "base"), (power, "power"),
                              (count, "count")):
                setup(v.tensor_copy(dst[:, :], const_of(name)))
            setup(v.memset(ones[:, :], 1.0))
            setup(v.memset(ones_row[:, :], 1.0))
            setup(v.memset(eps[:, :], EPS))
            setup.end()
            v.sem_inc(s_ready, 1)

            def reduce_slots(dst, src):
                return v.tensor_reduce(dst, src.rearrange("p k c -> p c k"), AX.X, ALU.max)

            def top_groups(step, src, left, dst, rounds):
                for r in range(rounds):
                    step(v.max(out=dst[:, 8 * r:8 * r + 8], in_=src))
                    step.settle()
                    if r < rounds - 1:
                        step(v.match_replace(out=left, in_to_replace=dst[:, 8 * r:8 * r + 8], in_values=src, imm_value=0.0))
                        step.settle()
                        src = left

            def expand(step, m):
                step(v.tensor_copy(tops_i[:, 0:m], tops[:, 0:m]))
                step.settle()
                step(v.tensor_scalar(tops_8[:, 0:m], tops_i[:, 0:m], BITS - 3, (2 * G - 1) * BITS,
                                     ALU.logical_shift_right, ALU.bitwise_and))
                step(v.tensor_tensor(set_bits[:, 0:m, :], tops_i[:, 0:m].unsqueeze(2).to_broadcast([P, m, BITS]),
                                     power[:, :].unsqueeze(1).to_broadcast([P, m, BITS]), ALU.bitwise_and))
                step.settle()
                step(v.tensor_tensor(numbered[:, 0:m, :], tops_8[:, 0:m].unsqueeze(2).to_broadcast([P, m, BITS]),
                                     const_of("bit").unsqueeze(1).to_broadcast([P, m, BITS]), ALU.subtract))
                step.settle()
                step(v.scalar_tensor_tensor(out=found[:, 0:m, :], in0=set_bits[:, 0:m, :], scalar=0.0,
                                            in1=numbered[:, 0:m, :], op0=ALU.not_equal, op1=ALU.mult))
                step.settle()

            flat = found[:, :, :].rearrange("p v k -> p (v k)")

            spare_tiles = v.alloc_register("tiles_through_the_spare_path")
            v.reg_mov(spare_tiles, 0)

            def spare(n, side):
                flag = v.value_load(spare_flag[0:1, bass.ds(n, 1)], min_val=0, max_val=CLS)
                with v.If(flag > 0):
                    with v.Fori(0, T) as t:
                        before = v.snap(spare_tiles, min_val=0, max_val=B * T - 1)
                        v.reg_add(spare_tiles, spare_tiles, 1)
                        step = Steps()
                        step(v.tensor_copy(sp_keys[:, :], keys[:, bass.ds(t, 1), :].rearrange("p a g -> p (a g)")))
                        step.settle()
                        top_groups(step, sp_keys[:, :], keys_left[:, :], tops, V0 // 8)
                        expand(step, V0)
                        top_groups(step, flat[:, 0:V0 * BITS], flat[:, 0:V0 * BITS], near, V0 // 8)
                        step(v.tensor_scalar(sp_index[:, :], near[:, 0:V0],
                                             const_of("offset")[:, bass.ds(n, 1)], None, ALU.add))
                        step.end()
                        v.sem_inc(s_spidx, 1)
                        step = Steps()
                        for i in range(S // SPARE):
                            v.wait_ge(s_sprows, before * (16 * S) + 16 * SPARE * (i + 1))
                            step(reduce_slots(head[:, i, :], sp_rows[:, :, :]))
                            step.settle()
                            if i < S // SPARE - 1:
                                v.sem_inc(s_spfree, 1)
                        step(v.tensor_reduce(sp_agg[:, side, bass.ds(t, 1), :].rearrange("p a c -> p (a c)"),
                                             head[:, 0:S // SPARE, :].rearrange("p k c -> p c k"), AX.X, ALU.max))
                        step.end()

            def make_mask(n):
                wait(v, s_packed, n)
                for q in range(4):
                    v.wait_ge(s_raw[q], 16 * (n + 1))
                    v.tensor_scalar(mask[:, 2 * q:2 * q + 2, :], raw[:, 2 * q:2 * q + 2, :], 0.0, None,
                                    ALU.not_equal).then_inc(s_mask, 1)

            def classify(n):
                step = Steps()
                v.wait_ge(s_bits, 3 * (n + 1))
                step(v.tensor_reduce(degree[:, :], bits[:, :, :, GB], AX.X, ALU.add))
                step.settle()
                step(v.tensor_scalar(cls[:, :], degree[:, :], float(CLS - 1), None, ALU.min))
                step.settle()
                a = cls[:, :].unsqueeze(2).to_broadcast([P, T, CLS])
                b = const_of("classes").unsqueeze(1).to_broadcast([P, T, CLS])
                step(v.tensor_tensor(same[:, :, :], a, b, ALU.is_equal))
                step(v.tensor_tensor(above[:, :, :], a, b, ALU.is_gt))
                step.end()
                v.sem_inc(s_class, 1)
                wait(v, s_sorted, 2 * n)
                v.scalar_tensor_tensor(out=high[:, :, :].rearrange("p t (j k) -> p t j k", k=GB),
                                       in0=bits[:, :, :, 0:GB], scalar=0.0,
                                       in1=base[:, :].rearrange("p (j k) -> p j k", k=GB).unsqueeze(1).to_broadcast([P, T, T, GB]),
                                       op0=ALU.is_gt, op1=ALU.mult).then_inc(s_high, 1)

            def make_perm(n):
                step = Steps()
                v.wait_ge(s_ranked, n + 1)
                step(v.tensor_tensor(picked[:, :, :], rank_ps[:, :, :], same[:, :, :], ALU.mult))
                v.tensor_copy(n_above[:, :], above_ps).then_inc(s_above, 1)
                step.settle()
                step(v.tensor_reduce(rank[:, :], picked[:, :, :], AX.X, ALU.add))
                step.settle()
                v.tensor_copy(rank16[:, :], rank[:, :]).then_inc(s_rank, 1)
                for t in range(T):
                    ins = v.tensor_scalar(perm[:, t, :], count[:, :], rank[:, t:t + 1], None, ALU.is_equal)
                    if t < T - 1:
                        step(ins)
                ins.then_inc(s_perm, 1)
                step.end()

            def find_neighbours(n, side):
                step = Steps()
                v.wait_ge(s_above, n + 1)
                v.wait_ge(s_keys, 2 * (n + 1))
                step(v.tensor_tensor(broken[:, :], n_above[:, :], const_of("limit"), ALU.is_gt))
                step(v.tensor_scalar(floor[:, bass.ds(n, 1), :].rearrange("p a t -> p (a t)"), const_of("node"),
                                     n_above[:, S:S + 1], -BIG, ALU.is_lt, ALU.mult))
                step.settle()
                step(v.tensor_reduce(n_broken[:, :], broken[:, :], AX.X, ALU.add))
                step.settle()
                step(v.tensor_copy(spare_flag[:, bass.ds(n, 1)], n_broken[:, :]))
                for t in range(1, T):
                    step(v.max(out=tops[:, V0 + V1 * (t - 1):V0 + V1 * t], in_=keys[:, t, :]))
                step.settle()
                top_groups(step, keys[:, 0, :], keys_left[:, :], tops, V0 // 8)
                expand(step, NV)
                for t in range(1, T):
                    step(v.max(out=near[:, V0 + V1 * (t - 1):V0 + V1 * t],
                               in_=flat[:, BITS * (V0 + V1 * (t - 1)):BITS * (V0 + V1 * t)]))
                top_groups(step, flat[:, 0:V0 * BITS], flat[:, 0:V0 * BITS], near, V0 // 8)
                a, h = FULL, P // 2
                step(v.tensor_copy(near[0:h, FOLD:FOLD + N_HALF], near[0:h, a:a + HALF:2]))
                step(v.tensor_copy(near[h:P, FOLD:FOLD + N_HALF], near[0:h, a + 1:a + HALF:2]))
                a, h = FULL + HALF, P // 4
                for s in range(4):
                    k = (QUARTER - s + 3) // 4
                    c0 = FOLD + N_HALF
                    step(v.tensor_copy(near[s * h:(s + 1) * h, c0:c0 + k], near[0:h, a + s:a + QUARTER:4]))
                    if k < N_QUARTER:
                        step(v.tensor_copy(near[s * h:(s + 1) * h, c0 + k:c0 + N_QUARTER], near[0:h, a:a + 1]))
                step.settle()
                step(v.tensor_scalar(index[:, side, :], near[:, :],
                                     const_of("offset")[:, bass.ds(n, 1)], None, ALU.add))
                step.end()
                v.sem_inc(s_index, 1)
                spare(n, side)
                v.sem_inc(s_extract, 1)

            def transpose_perm(n, side):
                v.wait_ge(s_row, n + 1)
                wait(v, s_turned, 2 * (n - 1))
                for t in range(SCALAR_TILES, T):
                    ins = v.tensor_scalar(perm_t[:, side, t, :],
                                          rank_row[:, side, :],
                                          const_of("node")[:, t:t + 1], None, ALU.is_equal)
                ins.then_inc(s_permt, 1)

            def reduce_head(n):
                step = Steps()
                wait(v, s_lo, n)
                v.wait_ge(s_rows[0], 16 * SLOTS[0] * (n + 1))
                r0, r1, r2 = FULL, FULL + N_HALF, SLOTS[0]
                step(reduce_slots(head[:, 0, :], rows[:, 0:r0, :]))
                step(reduce_slots(head[:, 1, :], rows[:, r0:r1, :]))
                step(reduce_slots(head[:, 3, :], rows[:, r1:r2, :]))
                step.settle()
                v.sem_inc(s_free[0], 1)
                step(v.tensor_copy(head[0:64, 2, :], head[64:128, 1, :]))
                for s in range(1, 4):
                    step(v.tensor_copy(head[0:32, 3 + s, :], head[32 * s:32 * s + 32, 3, :]))
                step.settle()
                step(v.tensor_copy(agg[64:128, 0, :], head[64:128, 0, :]))
                step(reduce_slots(agg[32:64, 0, :], head[32:64, 0:3, :]))
                step(reduce_slots(agg[0:32, 0, :], head[0:32, :, :]))
                step.end()

            def reduce_tiles(n, tiles):
                step = Steps()
                for t in tiles:
                    v.wait_ge(s_rows[t], 16 * SLOTS[t] * (n + 1))
                    src = rows[:, FIRST[t]:FIRST[t + 1], :]
                    if SLOTS[t] == 1:
                        ins = v.tensor_copy(agg[:, t, :], src[:, 0, :])
                    else:
                        ins = reduce_slots(agg[:, t, :], src)
                    step(ins)
                step.end()
                for t in tiles:
                    v.sem_inc(s_free[t], 1)

            def split_agg(n, side):
                step = Steps()
                flag = v.value_load(spare_flag[0:1, bass.ds(n, 1)], min_val=0, max_val=CLS)
                with v.If(flag > 0):
                    v.tensor_tensor(agg[:, :, :], agg[:, :, :],
                                    sp_agg[:, side, :, :],
                                    ALU.max).then_inc(s_step, 1)
                with v.Else():
                    v.sem_inc(s_step, 1)
                step.done += 1
                step.settle()
                v.sem_inc(s_agg, 1)
                v.wait_ge(s_hi, n + 1)
                for t in range(T):
                    ins = v.scalar_tensor_tensor(out=rest[:, t, :], in0=agg[:, t, :],
                                                 scalar=floor[:, bass.ds(n, 1), t],
                                                 in1=part[:, 0, t, :], op0=ALU.max, op1=ALU.subtract)
                    if t < T - 1:
                        step(ins)
                ins.then_inc(s_rest, 1)
                step.end()
                v.wait_ge(s_mid, n + 1)
                v.tensor_tensor(part[:, 2, :, :], rest[:, :, :], part[:, 1, :, :], ALU.subtract).then_inc(s_lo, 1)

            def layer_norm(n, h):
                step = Steps()
                tiles = range(4 * h, 4 * h + 4)
                v.wait_ge(s_x, 32 * (n + 1))
                v.wait_ge(s_lin, 2 * n + h + 1)
                wait(v, s_y, 2 * (n - 1) + h + 1)
                v.scalar_tensor_tensor(out=z[:, 4 * h:4 * h + 4, :], in0=out_ps[:, :].rearrange("p (t c) -> p t c", c=C),
                                       scalar=0.0, in1=x_in[:, 4 * h:4 * h + 4, :],
                                       op0=ALU.max, op1=ALU.add).then_inc(s_z, 1)
                v.wait_ge(s_z, 2 * n + h + 1)
                for t in tiles:
                    step(v.bn_stats(stats[:, t, :], z[:, t, :]))
                step.settle()
                for t in tiles:
                    ins = v.bn_aggr(mean_var[:, t, :], stats[:, t, :])
                    if t < tiles[-1]:
                        step(ins)
                ins.then_inc(s_var, 1)
                step.end()

            def invert(n, h):
                step = Steps()
                v.wait_ge(s_std, 2 * n + h + 1)
                step(v.reciprocal(inv_std[:, 4 * h:4 * h + 4], std[:, 4 * h:4 * h + 4]))
                step.end()
                v.scalar_tensor_tensor(out=shift[:, 4 * h:4 * h + 4], in0=mean_var[:, 4 * h:4 * h + 4, 0], scalar=-1.0,
                                       in1=inv_std[:, 4 * h:4 * h + 4], op0=ALU.mult, op1=ALU.mult).then_inc(s_inv, 1)

            def step_of(n, side, first=False, late=False, last=False):
                transpose_perm(n, side)
                if not last:
                    find_neighbours(n + 1, 1 - side)
                if not late:
                    make_mask(n + 2)
                if not first:
                    layer_norm(n - 1, 0)
                if not late:
                    classify(n + 2)
                if not first:
                    invert(n - 1, 0)
                reduce_head(n)
                reduce_tiles(n, [1])
                if not first:
                    layer_norm(n - 1, 1)
                if not late:
                    make_perm(n + 2)
                if not first:
                    invert(n - 1, 1)
                reduce_tiles(n, range(2, T))
                split_agg(n, side)

            for n in range(2):
                make_mask(n)
                classify(n)
                make_perm(n)
                if n == 0:
                    find_neighbours(0, 0)
            step_of(0, 0, first=True)
            step_of(1, 1)
            with v.Fori(1, B // 2 - 1) as pair:
                for side in range(2):
                    step_of(2 * pair + side, side)
            step_of(B - 2, 0, late=True)
            step_of(B - 1, 1, late=True, last=True)
            for h in range(2):
                layer_norm(B - 1, h)
                invert(B - 1, h)


_INS = ["x", "x_t", "table", "adj_t", "w", "bias", "const"]


def kernel(x, adj, L0_gnn_W, L0_gnn_b):
    import concourse.bacc as _bacc
    from concourse.bass_utils import run_bass_kernel_spmd as _run

    x = np.ascontiguousarray(x)
    arrays = {
        "x": x,
        "x_t": np.ascontiguousarray(x.transpose(0, 2, 1)),
        "table": np.concatenate([np.zeros((B, 1, C), x.dtype), x[:, ::-1]], axis=1).reshape(B * TABLE, C),
        "adj_t": np.ascontiguousarray(np.asarray(adj).transpose(0, 2, 1)),
        "w": np.ascontiguousarray(L0_gnn_W),
        "bias": np.ascontiguousarray(L0_gnn_b).reshape(1, C),
        "const": constants(),
    }
    nc = _bacc.Bacc("TRN2", target_bir_lowering=False, num_devices=1)
    args = [nc.dram_tensor(f"in_{k}", arrays[k].shape, mybir.dt.from_np(arrays[k].dtype), kind="ExternalInput").ap()
            for k in _INS]
    out = nc.dram_tensor("out_0", (B, N, C), F32, kind="ExternalOutput").ap()
    gnn_kernel(nc, *args, out)
    r = _run(nc, [{f"in_{k}": arrays[k] for k in _INS}], core_ids=[0])
    return r.results[0]["out_0"]
```

```python
from contextlib import ExitStack

import numpy as np

import concourse.bass as bass
from concourse import mybir

ALU = mybir.AluOpType
ACT = mybir.ActivationFunctionType
AX = mybir.AxisListType
F32 = mybir.dt.float32
F16 = mybir.dt.float16
BF16 = mybir.dt.bfloat16
I32 = mybir.dt.int32
U32 = mybir.dt.uint32

P = 128
B, N, C = 8, 1024, 128
S = 25
T = N // P
EPS = 1e-5
BIG = 3.0e38

BITS = 8
G = N // BITS
GB = P // BITS
PK = GB + 1
CLS = S + 2
TABLE = N + 1

FULL = 10
HALF = 4
QUARTER = S - FULL - HALF
N_HALF, N_QUARTER = HALF // 2, -(-QUARTER // 4)
SLOTS = [FULL + N_HALF + N_QUARTER, 7, 5, 4, 3, 3, 2, 1]
FIRST = [sum(SLOTS[:t]) for t in range(T + 1)]
LIMIT = [2.0 * N] * CLS
LIMIT[FULL], LIMIT[FULL + HALF] = P // 2, P // 4
for _t in range(T - 1, 0, -1):
    LIMIT[SLOTS[_t]] = min(LIMIT[SLOTS[_t]], _t * P)

V0 = 32
V1 = 8
NV = V0 + (T - 1) * V1
ORDER = list(range(2, T)) + [1]
GROUP = {}
_at = 0
for _t in ORDER:
    GROUP[_t] = _at
    _at += SLOTS[_t]
GROUP[0] = GROUP[1] + 8
NG = GROUP[0] + S
EARLY, LATE = [1, 2, 3], [4, 5, 6, 7]
SPARE = 5
NF = N_HALF + N_QUARTER
FOLD = NV

CONST = {}
_at = 0
for _name, _w in (("pack", PK), ("before", P), ("ident", P), ("base", G), ("classes", CLS),
                  ("limit", CLS), ("bit", BITS), ("power", BITS), ("offset", B), ("node", T), ("minus_node", T), ("count", N)):
    CONST[_name] = (_at, _at + _w)
    _at += _w
NCONST = _at


def constants():
    c = np.zeros((P, NCONST), np.float32)
    p = np.arange(P)

    def put(name, a):
        c[:, CONST[name][0]:CONST[name][1]] = a

    pack = np.zeros((P, PK), np.float32)
    pack[p, p // BITS] = 2.0 ** (p % BITS)
    pack[:, GB] = 1.0
    put("pack", pack)
    put("before", p[:, None] < p[None, :])
    put("ident", p[:, None] == p[None, :])
    put("base", (G - np.arange(G)) * 2.0 ** BITS)
    put("classes", np.arange(CLS))
    put("limit", np.array(LIMIT))
    put("bit", np.arange(BITS))
    put("power", 2.0 ** np.arange(BITS))
    put("offset", np.arange(B) * TABLE)
    put("node", p[:, None] + P * np.arange(T)[None, :])
    put("minus_node", -(p[:, None] + P * np.arange(T)[None, :]))
    put("count", np.arange(N))
    return c


def gnn_kernel(nc, x, x_t, table, adj_t, w, bias, const, out):
    with ExitStack() as ctx:
        def sb(name, shape, dt):
            return ctx.enter_context(nc.sbuf_tensor(name, shape, dt))

        def bank(name):
            return ctx.enter_context(nc.psum_tensor(name, [P, 512], F32))

        def sem(name):
            return ctx.enter_context(nc.semaphore(name))

        cst = sb("cst", [P, NCONST], F32)
        pack = sb("pack", [P, PK], BF16)
        before = sb("before", [P, P], BF16)
        ident = sb("ident", [P, P], F16)
        base = sb("base", [P, G], BF16)
        count = sb("count", [P, N], F16)
        power = sb("power", [P, BITS], I32)
        ones = sb("ones", [P, P], BF16)
        ones_row = sb("ones_row", [1, P], F32)
        eps = sb("eps", [P, 1], F32)
        w_self = sb("w_self", [P, C], F32)
        w_agg = sb("w_agg", [P, C], F32)
        bias_row = sb("bias_row", [1, C], F32)

        raw = sb("raw", [P, T, N], I32)
        mask = sb("mask", [P, T, N], BF16)
        bits = sb("bits", [P, T, T, PK], BF16)
        high = sb("high", [P, T, G], BF16)
        degree = sb("degree", [P, T], F32)
        cls = sb("cls", [P, T], F32)
        same = sb("same", [P, T, CLS], BF16)
        above = sb("above", [P, T, CLS], BF16)
        picked = sb("picked", [P, T, CLS], F32)
        rank = sb("rank", [P, T], F32)
        rank16 = sb("rank16", [P, T], F16)
        rank_row = sb("rank_row", [P, 2, N], F16)
        low = sb("low", [P, B], F32)
        distance = sb("distance", [P, 2, N], F16)
        n_above = sb("n_above", [P, CLS], F32)
        broken = sb("broken", [P, CLS], F32)
        n_broken = sb("n_broken", [P, 1], F32)
        spare_flag = sb("spare_flag", [P, B], I32)
        floor = sb("floor", [P, B, T], F32)
        perm = sb("perm", [P, T, N], BF16)
        perm_t = sb("perm_t", [P, 2, T, N], BF16)
        keys = sb("keys", [P, T, G], F32)
        keys_left = sb("keys_left", [P, G], F32)
        tops = sb("tops", [P, GROUP[0] + V0], F32)
        tops_i = sb("tops_i", [P, NG], I32)
        tops_8 = sb("tops_8", [P, NG], I32)
        numbered = sb("numbered", [P, NG, BITS], F32)
        set_bits = sb("set_bits", [P, NG, BITS], I32)
        found = sb("found", [P, NG, BITS], F32)
        near = sb("near", [P, NV + NF], F32)
        index = sb("index", [P, 2, NV + NF], U32)
        rows = sb("rows", [P, FIRST[T], C], F32)
        head = sb("head", [P, 7, C], F32)
        agg = sb("agg", [P, T, C], F32)
        rest = sb("rest", [P, T, C], F32)
        part = sb("part", [P, 3, T, C], BF16)
        agg_t = sb("agg_t", [P, N], F32)
        x_in = sb("x_in", [P, T, C], F32)
        xt_in = sb("xt_in", [P, N], F32)
        z = sb("z", [P, T, C], F32)
        stats = sb("stats", [P, T, 6], F32)
        mean_var = sb("mean_var", [P, T, 2], F32)
        std = sb("std", [P, T], F32)
        inv_std = sb("inv_std", [P, T], F32)
        shift = sb("shift", [P, T], F32)
        y = sb("y", [P, T, C], F32)
        sp_keys = sb("sp_keys", [P, G], F32)
        sp_index = sb("sp_index", [P, V0], U32)
        sp_rows = sb("sp_rows", [P, SPARE, C], F32)
        sp_agg = sb("sp_agg", [P, 2, T, C], F32)

        banks = [bank(f"bank{i}") for i in range(8)]
        PER = [3, 3, 2]

        def bits_ps(i):
            return banks[i][:, 0:PER[i] * T * PK].rearrange("p (t j k) -> p t j k", t=PER[i], k=PK)

        rank_ps = banks[3][:, 0:T * CLS].rearrange("p (t d) -> p t d", t=T)
        above_ps = banks[3][:, T * CLS:(T + 1) * CLS]
        aggt_ps = (banks[6], banks[3])
        out_ps = (banks[7], banks[2])

        s_const = sem("constants_loaded")
        s_ready = sem("constants_made")
        s_raw = [sem(f"raw_loaded_{q}") for q in range(4)]
        s_mask = sem("mask_made")
        s_packed = sem("bits_packed")
        s_bits = sem("bits_copied")
        s_high = sem("high_made")
        s_class = sem("classes_made")
        s_ranked = sem("rank_sums_made")
        s_rank = sem("rank_made")
        s_above = sem("above_kept")
        s_row_ps = sem("rank_row_made")
        s_row = sem("rank_row_copied")
        s_perm = sem("perm_made")
        s_sorted = sem("keys_sorted")
        s_keys = sem("keys_copied")
        s_extract = sem("keys_used")
        s_index = sem("index_made")
        s_rows = [sem(f"rows_gathered_{t}") for t in range(T)]
        s_reduced = sem("rows_reduced")
        s_free = [sem(f"rows_free_{t}") for t in range(T)]
        s_agg = sem("agg_made")
        s_hi = sem("hi_made")
        s_rest = sem("rest_made")
        s_mid = sem("mid_made")
        s_lo = sem("lo_made")
        s_permt = sem("perm_t_made")
        s_distance = sem("distance_made")
        s_turned = sem("agg_turned")
        s_aggt = sem("agg_t_copied")
        s_x = sem("x_loaded")
        s_lin = sem("linear_made")
        s_z = sem("z_made")
        s_var = sem("variance_made")
        s_std = sem("std_made")
        s_inv = sem("inverse_std_made")
        s_y = sem("y_made")
        s_out = [sem(f"out_stored_{h}") for h in range(2)]
        s_spidx = sem("spare_index_made")
        s_sprows = sem("spare_rows_gathered")
        s_spfree = sem("spare_rows_free")
        s_step = sem("vector_steps")

        def wait(eng, s, value):
            if not isinstance(value, int) or value > 0:
                eng.wait_ge(s, value)

        block = ctx.enter_context(nc.Block())


        @block.sync
        def _(sp):
            sp.dma_start(cst[:, :], const).then_inc(s_const, 16)
            sp.dma_start(w_self[:, :], w[0:C, :]).then_inc(s_const, 16)
            sp.dma_start(w_agg[:, :], w[C:2 * C, :]).then_inc(s_const, 16)
            sp.dma_start(bias_row[:, :], bias).then_inc(s_const, 16)

            def load_adj(n):
                for q in range(4):
                    wait(sp, s_mask, 4 * (n - 1) + q + 1)
                    sp.dma_start(raw[:, 2 * q:2 * q + 2, :],
                                 adj_t[bass.ds(n, 1), 2 * q * P:(2 * q + 2) * P, :]
                                 .rearrange("a (j p) i -> p (a j) i", p=P)).then_inc(s_raw[q], 16)

            def load_x(n):
                wait(sp, s_z, 2 * n)
                wait(sp, s_lin, 2 * n)
                sp.dma_start(x_in[:, :, :], x[bass.ds(n, 1), :, :].rearrange("a (t p) c -> p (a t) c", p=P)).then_inc(s_x, 16)
                sp.dma_start(xt_in[:, :], x_t[bass.ds(n, 1), :, :].rearrange("a c i -> c (a i)")).then_inc(s_x, 16)

            for n in range(3):
                load_adj(n)
            load_x(0)
            load_adj(3)
            with sp.Fori(1, B - 3) as n:
                load_adj(n + 3)
                load_x(n)
            for n in range(B - 3, B):
                load_x(n)

        @block.gpsimd
        def _(pool):
            def gather(dst, idx, done):
                pool.indirect_dma_start(dst, None, table, bass.IndirectOffsetOnAxis(ap=idx, axis=0)).then_inc(done, 16)

            def spare(n):
                flag = pool.value_load(spare_flag[0:1, bass.ds(n, 1)], min_val=0, max_val=CLS)
                with pool.If(flag > 0):
                    with pool.Fori(0, T):
                        pool.wait_ge(s_spidx, 1)
                        pool.sem_clear(s_spidx)
                        for k in range(S):
                            if k % SPARE == 0 and k > 0:
                                pool.wait_ge(s_spfree, 1)
                                pool.sem_clear(s_spfree)
                            gather(sp_rows[:, k % SPARE, :], sp_index[:, k:k + 1], s_sprows)

            def gathers(n, side):
                pool.wait_ge(s_index, n + 1)
                spare(n)
                for t in range(T):
                    if not isinstance(n, int) or n > 0:
                        pool.wait_ge(s_free[t], 1)
                        pool.sem_clear(s_free[t])
                    columns = (list(range(FULL)) + list(range(FOLD, FOLD + NF)) if t == 0 else
                               [V0 + V1 * (t - 1) + k for k in range(SLOTS[t])])
                    for k, col in enumerate(columns):
                        gather(rows[:, FIRST[t] + k, :], index[:, side, col:col + 1], s_rows[t])

            gathers(0, 0)
            gathers(1, 1)
            with pool.Fori(1, B // 2) as pair:
                gathers(2 * pair, 0)
                gathers(2 * pair + 1, 1)

        @block.tensor
        def _(pe):
            def pack_bits(n):
                if isinstance(n, int) and n == 0:
                    pe.wait_ge(s_ready, 1)
                wait(pe, s_row, n)
                wait(pe, s_class, n)
                wait(pe, s_bits, 3 * n)
                wait(pe, s_z, 2 * (n - 3))
                for j in range(T):
                    if j % 2 == 0:
                        pe.wait_ge(s_mask, 4 * n + j // 2 + 1)
                    for t in range(T):
                        last = nc.tensor.matmul(bits_ps(t // 3)[:, t % 3, j, :], mask[:, j, t * P:(t + 1) * P],
                                                pack[:, :], start=True, stop=True)
                last.then_inc(s_packed, 1)

            def rank_nodes(n):
                pe.wait_ge(s_class, n + 1)
                wait(pe, s_above, n)
                wait(pe, s_rank, n)
                wait(pe, s_aggt, 2 * (n - 3))
                nc.tensor.matmul(rank_ps[:, :, :], before[:, :], same[:, :, :], start=True, stop=False)
                for t in range(T - 1):
                    nc.tensor.matmul(rank_ps[:, t + 1:, :], ones[:, :],
                                     same[:, t:t + 1, :].to_broadcast([P, T - 1 - t, CLS]), start=False, stop=False)
                for t in range(T):
                    nc.tensor.matmul(rank_ps[:, :, :], ones[:, :], above[:, t:t + 1, :].to_broadcast([P, T, CLS]),
                                     start=False, stop=(t == T - 1))
                for t in range(T):
                    last = nc.tensor.matmul(above_ps, ones[:, :], above[:, t, :], start=(t == 0), stop=(t == T - 1))
                last.then_inc(s_ranked, 1)

            def spread_rank(n):
                pe.wait_ge(s_rank, n + 1)
                pe.wait_ge(s_bits, 3 * (n + 1))
                for t in range(T):
                    last = nc.tensor.matmul(banks[t // 4][:, (t % 4) * P:(t % 4 + 1) * P],
                                            rank16[:, t:t + 1].to_broadcast([P, P]), ident[:, :], start=True, stop=True)
                last.then_inc(s_row_ps, 1)

            def sort_keys(n):
                wait(pe, s_keys, 2 * n)
                pe.wait_ge(s_high, n + 1)
                pe.wait_ge(s_perm, n + 1)
                for r in range(T):
                    dst = banks[4 + r // 4][:, (r % 4) * G:(r % 4 + 1) * G]
                    for t in range(T):
                        weights = perm[:, t, r * P:(r + 1) * P]
                        nc.tensor.matmul(dst, weights, bits[:, t, :, 0:GB], start=(t == 0), stop=False)
                        last = nc.tensor.matmul(dst, weights, high[:, t, :], start=False, stop=(t == T - 1))
                    if r % 4 == 3:
                        last.then_inc(s_sorted, 1)

            def turn_agg(n, side, h, newest):
                if h == 0:
                    pe.wait_ge(s_permt, T * (n + 1))
                    pe.wait_ge(s_hi, n + 1)
                    pe.wait_ge(s_mid, n + 1)
                    pe.wait_ge(s_lo, n + 1)
                    wait(pe, s_aggt, 2 * n - 1)
                else:
                    wait(pe, s_aggt, 2 * n)
                    pe.wait_ge(s_rank, newest + 1)
                    pe.wait_ge(s_above, newest + 1)
                for r in range(T):
                    turned = perm_t[:, side, r, h * 512:(h + 1) * 512]
                    for k in range(3):
                        last = nc.tensor.matmul(aggt_ps[h][:, :], part[:, k, r, :], turned,
                                                start=(r == 0 and k == 0), stop=(r == T - 1 and k == 2))
                last.then_inc(s_turned, 1)

            def linear(n, h, newest):
                pe.wait_ge(s_x, 32 * (n + 1))
                pe.wait_ge(s_aggt, 2 * n + h + 1)
                wait(pe, s_z, 2 * n + h - 1)
                if h == 1:
                    pe.wait_ge(s_bits, 3 * (newest + 1))
                for t in range(4 * h, 4 * h + 4):
                    dst = out_ps[h][:, (t % 4) * C:(t % 4 + 1) * C]
                    nc.tensor.matmul(dst, ones_row[:, :], bias_row[:, :], start=True, stop=False)
                    nc.tensor.matmul(dst, xt_in[:, t * P:(t + 1) * P], w_self[:, :], start=False, stop=False)
                    last = nc.tensor.matmul(dst, agg_t[:, t * P:(t + 1) * P], w_agg[:, :], start=False, stop=True)
                last.then_inc(s_lin, 1)

            def step(n, side, first=False, late=False):
                newest = B - 1 if late else n + 2
                if not late:
                    pack_bits(n + 2)
                    rank_nodes(n + 2)
                if not first:
                    for h in range(2):
                        turn_agg(n - 1, 1 - side, h, newest)
                if not late:
                    spread_rank(n + 2)
                if not first:
                    for h in range(2):
                        linear(n - 1, h, newest)
                if not late:
                    sort_keys(n + 2)

            for n in range(2):
                pack_bits(n)
                rank_nodes(n)
                spread_rank(n)
                sort_keys(n)
            step(0, 0, first=True)
            step(1, 1)
            with pe.Fori(1, B // 2 - 1) as pair:
                for side in range(2):
                    step(2 * pair + side, side)
            for n in range(B - 2, B + 1):
                step(n, n % 2, late=True)

        @block.scalar
        def _(act):
            def copy_bits(n):
                act.wait_ge(s_packed, n + 1)
                wait(act, s_sorted, 2 * n)
                for i in range(3):
                    nc.scalar.copy(bits[:, 3 * i:3 * i + PER[i], :, :], bits_ps(i)).then_inc(s_bits, 1)

            def copy_ranks(n, side):
                act.wait_ge(s_row_ps, n + 1)
                wait(act, s_permt, T * (n - 1))
                for h in range(2):
                    ins = nc.scalar.copy(rank_row[:, side, h * 512:(h + 1) * 512], banks[h][:, :])
                ins.then_inc(s_row, 1)

            def copy_keys(n):
                wait(act, s_extract, n)
                for h in range(2):
                    act.wait_ge(s_sorted, 2 * n + h + 1)
                    nc.scalar.copy(keys[:, 4 * h:4 * h + 4, :].rearrange("p t g -> p (t g)"),
                                   banks[4 + h][:, :]).then_inc(s_keys, 1)

            def high_part(n):
                act.wait_ge(s_agg, n + 1)
                wait(act, s_turned, 2 * n)
                nc.scalar.copy(part[:, 0, :, :], agg[:, :, :]).then_inc(s_hi, 1)

            def middle_part(n):
                act.wait_ge(s_rest, n + 1)
                nc.scalar.copy(part[:, 1, :, :], rest[:, :, :]).then_inc(s_mid, 1)

            def transpose_perm(n, side, tiles):
                act.wait_ge(s_row, n + 1)
                wait(act, s_turned, 2 * (n - 1))
                for t in tiles:
                    wait(act, s_permt, T * n + t - 1)
                    nc.scalar.activation(distance[:, t % 2, :], rank_row[:, side, :],
                                         ACT.Abs, bias=cst[:, CONST["minus_node"][0] + t:CONST["minus_node"][0] + t + 1]
                                         ).then_inc(s_distance, 1)
                    act.wait_ge(s_distance, T * n + t + 1)
                    nc.scalar.activation(perm_t[:, side, t, :], distance[:, t % 2, :],
                                         ACT.Relu, bias=1.0, scale=-1.0).then_inc(s_permt, 1)

            def copy_turned(n, h):
                act.wait_ge(s_turned, 2 * n + h + 1)
                wait(act, s_lin, 2 * (n - 1) + h + 1)
                nc.scalar.copy(agg_t[:, h * 512:(h + 1) * 512], aggt_ps[h][:, :]).then_inc(s_aggt, 1)

            def root(n, h):
                act.wait_ge(s_var, 2 * n + h + 1)
                nc.scalar.activation(std[:, 4 * h:4 * h + 4], mean_var[:, 4 * h:4 * h + 4, 1], ACT.Sqrt,
                                     bias=eps[:, 0:1]).then_inc(s_std, 1)

            def normalise(n, h):
                act.wait_ge(s_inv, 2 * n + h + 1)
                wait(act, s_out[h], 16 * n)
                for t in range(4 * h, 4 * h + 4):
                    ins = nc.scalar.activation(y[:, t, :], z[:, t, :], ACT.Identity, bias=shift[:, t:t + 1],
                                               scale=inv_std[:, t:t + 1])
                ins.then_inc(s_y, 1)
                act.wait_ge(s_y, 2 * n + h + 1)
                act.dma_start(out[bass.ds(n, 1), h * 512:(h + 1) * 512, :].rearrange("a (t p) c -> p (a t) c", p=P),
                              y[:, 4 * h:4 * h + 4, :]).then_inc(s_out[h], 16)

            def step(n, side, first=False, late=False):
                if not first:
                    high_part(n - 1)
                if not late:
                    copy_bits(n + 2)
                if not first:
                    middle_part(n - 1)
                transpose_perm(n, side, range(0, 3))
                if not first:
                    copy_turned(n - 1, 0)
                transpose_perm(n, side, range(3, 5))
                if not first:
                    copy_turned(n - 1, 1)
                transpose_perm(n, side, range(5, T))
                if not late:
                    copy_ranks(n + 2, side)
                if not first:
                    for h in range(2):
                        root(n - 1, h)
                    for h in range(2):
                        normalise(n - 1, h)
                if not late:
                    copy_keys(n + 2)

            act.wait_ge(s_ready, 1)
            for n in range(2):
                copy_bits(n)
                copy_ranks(n, n)
                copy_keys(n)
            step(0, 0, first=True)
            step(1, 1)
            with act.Fori(1, B // 2 - 1) as pair:
                for side in range(2):
                    step(2 * pair + side, side)
            step(B - 2, 0, late=True)
            step(B - 1, 1, late=True)
            high_part(B - 1)
            middle_part(B - 1)
            for h in range(2):
                copy_turned(B - 1, h)
            for h in range(2):
                root(B - 1, h)
            for h in range(2):
                normalise(B - 1, h)
            for h in range(2):
                act.wait_ge(s_out[h], 16 * B)

        @block.vector
        def _(v):
            def const_of(name):
                return cst[:, CONST[name][0]:CONST[name][1]]

            class Steps:

                def __init__(self):
                    self.done = 0

                def __call__(self, ins):
                    ins.then_inc(s_step, 1)
                    self.done += 1
                    return self.done

                def settle(self, upto=None):
                    v.wait_ge(s_step, self.done if upto is None else upto)

                def end(self):
                    self.settle()
                    v.sem_clear(s_step)

            v.wait_ge(s_const, 64)
            setup = Steps()
            for dst, name in ((pack, "pack"), (before, "before"), (ident, "ident"), (base, "base"), (power, "power"),
                              (count, "count")):
                setup(v.tensor_copy(dst[:, :], const_of(name)))
            setup(v.memset(ones[:, :], 1.0))
            setup(v.memset(ones_row[:, :], 1.0))
            setup(v.memset(eps[:, :], EPS))
            setup.end()
            v.sem_inc(s_ready, 1)

            def reduce_slots(dst, src):
                return v.tensor_reduce(dst, src.rearrange("p k c -> p c k"), AX.X, ALU.max)

            def top_eights(step, src, left, dst, rounds, others=()):
                others = list(others)
                for r in range(rounds):
                    for half in range(1 if r == rounds - 1 else 2):
                        if half == 0:
                            made = step(v.max(out=dst[:, 8 * r:8 * r + 8], in_=src))
                        else:
                            made = step(v.match_replace(out=left, in_to_replace=dst[:, 8 * r:8 * r + 8], in_values=src,
                                                        imm_value=0.0))
                            src = left
                        if others:
                            step.settle(made - 1)
                            step(others.pop(0)())
                        step.settle(made)
                assert not others

            def expand(step, a, b):
                m = b - a
                step(v.tensor_copy(tops_i[:, a:b], tops[:, a:b]))
                step.settle()
                step(v.tensor_scalar(tops_8[:, a:b], tops_i[:, a:b], BITS - 3, (2 * G - 1) * BITS,
                                     ALU.logical_shift_right, ALU.bitwise_and))
                step(v.tensor_tensor(set_bits[:, a:b, :], tops_i[:, a:b].unsqueeze(2).to_broadcast([P, m, BITS]),
                                     power[:, :].unsqueeze(1).to_broadcast([P, m, BITS]), ALU.bitwise_and))
                step.settle(step.done - 1)
                step(v.tensor_tensor(numbered[:, a:b, :], tops_8[:, a:b].unsqueeze(2).to_broadcast([P, m, BITS]),
                                     const_of("bit").unsqueeze(1).to_broadcast([P, m, BITS]), ALU.subtract))
                step.settle()
                step(v.scalar_tensor_tensor(out=found[:, a:b, :], in0=set_bits[:, a:b, :], scalar=0.0,
                                            in1=numbered[:, a:b, :], op0=ALU.not_equal, op1=ALU.mult))
                step.settle()

            flat = found[:, :, :].rearrange("p v k -> p (v k)")
            flat_0 = flat[:, GROUP[0] * BITS:NG * BITS]

            spare_tiles = v.alloc_register("tiles_through_the_spare_path")
            v.reg_mov(spare_tiles, 0)

            def spare(n, side):
                flag = v.value_load(spare_flag[0:1, bass.ds(n, 1)], min_val=0, max_val=CLS)
                with v.If(flag > 0):
                    with v.Fori(0, T) as t:
                        before = v.snap(spare_tiles, min_val=0, max_val=B * T - 1)
                        v.reg_add(spare_tiles, spare_tiles, 1)
                        step = Steps()
                        step(v.tensor_copy(sp_keys[:, :], keys[:, bass.ds(t, 1), :].rearrange("p a g -> p (a g)")))
                        step.settle()
                        top_eights(step, sp_keys[:, :], keys_left[:, :], tops[:, GROUP[0]:], V0 // 8)
                        expand(step, GROUP[0], NG)
                        top_eights(step, flat_0, flat_0, near, V0 // 8)
                        step(v.tensor_scalar(sp_index[:, :], near[:, 0:V0],
                                             const_of("offset")[:, bass.ds(n, 1)], None, ALU.add))
                        step.end()
                        v.sem_inc(s_spidx, 1)
                        step = Steps()
                        for i in range(S // SPARE):
                            v.wait_ge(s_sprows, before * (16 * S) + 16 * SPARE * (i + 1))
                            step(reduce_slots(head[:, i, :], sp_rows[:, :, :]))
                            step.settle()
                            if i < S // SPARE - 1:
                                v.sem_inc(s_spfree, 1)
                        step(v.tensor_reduce(sp_agg[:, side, bass.ds(t, 1), :].rearrange("p a c -> p (a c)"),
                                             head[:, 0:S // SPARE, :].rearrange("p k c -> p c k"), AX.X, ALU.max))
                        step.end()

            def make_mask(n):
                wait(v, s_packed, n)
                for q in range(4):
                    v.wait_ge(s_raw[q], 16 * (n + 1))
                    v.tensor_scalar(mask[:, 2 * q:2 * q + 2, :], raw[:, 2 * q:2 * q + 2, :], 0.0, None,
                                    ALU.not_equal).then_inc(s_mask, 1)

            def classify(n):
                step = Steps()
                v.wait_ge(s_bits, 3 * (n + 1))
                step(v.tensor_reduce(degree[:, :], bits[:, :, :, GB], AX.X, ALU.add))
                step.settle()
                step(v.tensor_scalar(cls[:, :], degree[:, :], float(CLS - 1), None, ALU.min))
                step.settle()
                a = cls[:, :].unsqueeze(2).to_broadcast([P, T, CLS])
                b = const_of("classes").unsqueeze(1).to_broadcast([P, T, CLS])
                step(v.tensor_tensor(same[:, :, :], a, b, ALU.is_equal))
                step(v.tensor_tensor(above[:, :, :], a, b, ALU.is_gt))
                step.end()
                v.sem_inc(s_class, 1)
                wait(v, s_sorted, 2 * n)
                v.scalar_tensor_tensor(out=high[:, :, :].rearrange("p t (j k) -> p t j k", k=GB),
                                       in0=bits[:, :, :, 0:GB], scalar=0.0,
                                       in1=base[:, :].rearrange("p (j k) -> p j k", k=GB).unsqueeze(1).to_broadcast([P, T, T, GB]),
                                       op0=ALU.is_gt, op1=ALU.mult).then_inc(s_high, 1)

            def make_perm(n):
                step = Steps()
                v.wait_ge(s_ranked, n + 1)
                step(v.tensor_tensor(picked[:, :, :], rank_ps[:, :, :], same[:, :, :], ALU.mult))
                v.tensor_copy(n_above[:, :], above_ps).then_inc(s_above, 1)
                step.settle()
                step(v.tensor_reduce(rank[:, :], picked[:, :, :], AX.X, ALU.add))
                step.settle()
                v.tensor_copy(rank16[:, :], rank[:, :]).then_inc(s_rank, 1)
                for t in range(T):
                    ins = v.tensor_scalar(perm[:, t, :], count[:, :], rank[:, t:t + 1], None, ALU.is_equal)
                    if t < T - 1:
                        step(ins)
                ins.then_inc(s_perm, 1)
                step.end()

            def best_groups(n):
                step = Steps()
                v.wait_ge(s_above, n + 1)
                a = step(v.tensor_tensor(broken[:, :], n_above[:, :], const_of("limit"), ALU.is_gt))
                step(v.tensor_scalar(floor[:, bass.ds(n, 1), :].rearrange("p a t -> p (a t)"), const_of("node"),
                                     n_above[:, S:S + 1], -BIG, ALU.is_lt, ALU.mult))
                step.settle(a)
                v.wait_ge(s_keys, 2 * (n + 1))
                a = step(v.tensor_reduce(n_broken[:, :], broken[:, :], AX.X, ALU.add))
                step.settle()
                step(v.tensor_copy(spare_flag[:, bass.ds(n, 1)], n_broken[:, :]))
                step(v.tensor_scalar(low[:, bass.ds(n, 1)], n_broken[:, :], 0.0, -BIG, ALU.is_gt, ALU.mult))
                top_eights(step, keys[:, 0, :], keys_left[:, :], tops[:, GROUP[0]:], V0 // 8,
                           [lambda t=t: v.max(out=tops[:, GROUP[t]:GROUP[t] + 8], in_=keys[:, t, :]) for t in ORDER])
                step.end()

            def make_index(n, side):
                step = Steps()
                top_eights(step, flat_0, flat_0, near, V0 // 8,
                           [lambda t=t: v.max(out=near[:, V0 + V1 * (t - 1):V0 + V1 * t],
                                              in_=flat[:, BITS * GROUP[t]:BITS * (GROUP[t] + SLOTS[t])])
                            for t in range(1, T)])
                a, h = FULL, P // 2
                step(v.tensor_copy(near[0:h, FOLD:FOLD + N_HALF], near[0:h, a:a + HALF:2]))
                step(v.tensor_copy(near[h:P, FOLD:FOLD + N_HALF], near[0:h, a + 1:a + HALF:2]))
                a, h = FULL + HALF, P // 4
                for s in range(4):
                    k = (QUARTER - s + 3) // 4
                    c0 = FOLD + N_HALF
                    step(v.tensor_copy(near[s * h:(s + 1) * h, c0:c0 + k], near[0:h, a + s:a + QUARTER:4]))
                    if k < N_QUARTER:
                        step(v.tensor_copy(near[s * h:(s + 1) * h, c0 + k:c0 + N_QUARTER], near[0:h, a:a + 1]))
                step.settle()
                step(v.tensor_scalar(index[:, side, :], near[:, :],
                                     const_of("offset")[:, bass.ds(n, 1)], None, ALU.add))
                step.end()
                v.sem_inc(s_index, 1)
                spare(n, side)
                v.sem_inc(s_extract, 1)

            def reduce_head(n):
                step = Steps()
                wait(v, s_lo, n)
                v.wait_ge(s_rows[0], 16 * SLOTS[0] * (n + 1))
                r0, r1, r2 = FULL, FULL + N_HALF, SLOTS[0]
                step(reduce_slots(head[:, 0, :], rows[:, 0:r0, :]))
                step(reduce_slots(head[:, 1, :], rows[:, r0:r1, :]))
                step(reduce_slots(head[:, 3, :], rows[:, r1:r2, :]))
                step.settle()
                v.sem_inc(s_free[0], 1)
                step(v.tensor_copy(head[0:64, 2, :], head[64:128, 1, :]))
                for s in range(1, 4):
                    step(v.tensor_copy(head[0:32, 3 + s, :], head[32 * s:32 * s + 32, 3, :]))
                step.settle()
                step(v.tensor_copy(agg[64:128, 0, :], head[64:128, 0, :]))
                step(reduce_slots(agg[32:64, 0, :], head[32:64, 0:3, :]))
                step(reduce_slots(agg[0:32, 0, :], head[0:32, :, :]))
                step.end()

            def reduce_tiles(n, tiles):
                step = Steps()
                for t in tiles:
                    v.wait_ge(s_rows[t], 16 * SLOTS[t] * (n + 1))
                    src = rows[:, FIRST[t]:FIRST[t + 1], :]
                    if SLOTS[t] == 1:
                        ins = v.tensor_copy(agg[:, t, :], src[:, 0, :])
                    else:
                        ins = reduce_slots(agg[:, t, :], src)
                    step(ins)
                step.end()
                for t in tiles:
                    v.sem_inc(s_free[t], 1)

            def finish_agg(n, side, flag):
                reduce_tiles(n, LATE)
                step = Steps()
                with v.If(flag > 0):
                    v.tensor_tensor(agg[:, :, :], agg[:, :, :], sp_agg[:, side, :, :], ALU.max).then_inc(s_step, 1)
                    v.wait_ge(s_step, 1)
                    for t in range(1, T):
                        v.tensor_scalar(agg[:, t, :], agg[:, t, :], floor[:, bass.ds(n, 1), t], None,
                                        ALU.max).then_inc(s_step, 1)
                with v.Else():
                    v.sem_inc(s_step, T)
                step.done += T
                step.end()
                v.sem_inc(s_agg, 1)

            def split_rest(n):
                v.wait_ge(s_hi, n + 1)
                step = Steps()
                for scalar, a, b in ((floor[:, bass.ds(n, 1), 0], 0, 1), (low[:, bass.ds(n, 1)], 1, T)):
                    ins = v.scalar_tensor_tensor(out=rest[:, a:b, :], in0=agg[:, a:b, :], scalar=scalar,
                                                 in1=part[:, 0, a:b, :], op0=ALU.max, op1=ALU.subtract)
                    if b < T:
                        step(ins)
                ins.then_inc(s_rest, 1)
                step.end()

            def split_low(n):
                v.wait_ge(s_mid, n + 1)
                v.tensor_tensor(part[:, 2, :, :], rest[:, :, :], part[:, 1, :, :], ALU.subtract).then_inc(s_lo, 1)

            def layer_norm(n, h):
                step = Steps()
                tiles = range(4 * h, 4 * h + 4)
                v.wait_ge(s_x, 32 * (n + 1))
                v.wait_ge(s_lin, 2 * n + h + 1)
                wait(v, s_y, 2 * (n - 1) + h + 1)
                v.scalar_tensor_tensor(out=z[:, 4 * h:4 * h + 4, :], in0=out_ps[h][:, :].rearrange("p (t c) -> p t c", c=C),
                                       scalar=0.0, in1=x_in[:, 4 * h:4 * h + 4, :],
                                       op0=ALU.max, op1=ALU.add).then_inc(s_z, 1)
                v.wait_ge(s_z, 2 * n + h + 1)
                for t in tiles:
                    step(v.bn_stats(stats[:, t, :], z[:, t, :]))
                step.settle()
                for t in tiles:
                    ins = v.bn_aggr(mean_var[:, t, :], stats[:, t, :])
                    if t < tiles[-1]:
                        step(ins)
                ins.then_inc(s_var, 1)
                step.end()

            def invert(n, h):
                step = Steps()
                v.wait_ge(s_std, 2 * n + h + 1)
                step(v.reciprocal(inv_std[:, 4 * h:4 * h + 4], std[:, 4 * h:4 * h + 4]))
                step.end()
                v.scalar_tensor_tensor(out=shift[:, 4 * h:4 * h + 4], in0=mean_var[:, 4 * h:4 * h + 4, 0], scalar=-1.0,
                                       in1=inv_std[:, 4 * h:4 * h + 4], op0=ALU.mult, op1=ALU.mult).then_inc(s_inv, 1)

            def step_of(n, side, first=False, late=False, last=False, done=False):
                if not first:
                    flag = v.value_load(spare_flag[0:1, bass.ds(n - 1, 1)], min_val=0, max_val=CLS)
                if not late:
                    make_mask(n + 2)
                if not first:
                    finish_agg(n - 1, 1 - side, flag)
                if not last:
                    best_groups(n + 1)
                if not first:
                    split_rest(n - 1)
                if not late:
                    classify(n + 2)
                if not first:
                    split_low(n - 1)
                if not last:
                    expand_all()
                if not late:
                    make_perm(n + 2)
                if not last:
                    make_index(n + 1, 1 - side)
                if not done:
                    reduce_head(n)
                if not first:
                    layer_norm(n - 1, 0)
                if not done:
                    reduce_tiles(n, EARLY[:2])
                if not first:
                    layer_norm(n - 1, 1)
                    for h in range(2):
                        invert(n - 1, h)
                if not done:
                    reduce_tiles(n, EARLY[2:])

            def expand_all():
                step = Steps()
                expand(step, 0, NG)
                step.end()

            make_mask(0)
            classify(0)
            make_perm(0)
            make_mask(1)
            best_groups(0)
            expand_all()
            make_index(0, 0)
            classify(1)
            make_perm(1)
            step_of(0, 0, first=True)
            step_of(1, 1)
            with v.Fori(1, B // 2 - 1) as pair:
                for side in range(2):
                    step_of(2 * pair + side, side)
            step_of(B - 2, 0, late=True)
            step_of(B - 1, 1, late=True, last=True)
            step_of(B, 0, late=True, last=True, done=True)


_INS = ["x", "x_t", "table", "adj_t", "w", "bias", "const"]


def kernel(x, adj, L0_gnn_W, L0_gnn_b):
    import concourse.bacc as _bacc
    from concourse.bass_utils import run_bass_kernel_spmd as _run

    x = np.ascontiguousarray(x)
    arrays = {
        "x": x,
        "x_t": np.ascontiguousarray(x.transpose(0, 2, 1)),
        "table": np.concatenate([np.zeros((B, 1, C), x.dtype), x[:, ::-1]], axis=1).reshape(B * TABLE, C),
        "adj_t": np.ascontiguousarray(np.asarray(adj).transpose(0, 2, 1)),
        "w": np.ascontiguousarray(L0_gnn_W),
        "bias": np.ascontiguousarray(L0_gnn_b).reshape(1, C),
        "const": constants(),
    }
    nc = _bacc.Bacc("TRN2", target_bir_lowering=False, num_devices=1)
    args = [nc.dram_tensor(f"in_{k}", arrays[k].shape, mybir.dt.from_np(arrays[k].dtype), kind="ExternalInput").ap()
            for k in _INS]
    out = nc.dram_tensor("out_0", (B, N, C), F32, kind="ExternalOutput").ap()
    gnn_kernel(nc, *args, out)
    r = _run(nc, [{f"in_{k}": arrays[k] for k in _INS}], core_ids=[0])
    return r.results[0]["out_0"]
```

```python
from contextlib import ExitStack

import numpy as np

import concourse.bass as bass
from concourse import mybir

ALU = mybir.AluOpType
ACT = mybir.ActivationFunctionType
AX = mybir.AxisListType
F32 = mybir.dt.float32
F16 = mybir.dt.float16
BF16 = mybir.dt.bfloat16
I32 = mybir.dt.int32
U32 = mybir.dt.uint32

P = 128
B, N, C = 8, 1024, 128
S = 25
T = N // P
HN = N // 2
EPS = 1e-5
BIG = 3.0e38

BITS = 8
G = N // BITS
GB = P // BITS
PK = GB + 1
CLS = S + 2
TABLE = N + 1

FULL = 8
HALF = 6
QUARTER = S - FULL - HALF
N_HALF, N_QUARTER = HALF // 2, (QUARTER + 1) // 4
QUADRANTS = [0, 1, 3, 2]
THIRD = slice(2 * P // 4, 3 * P // 4)
SLOTS = [FULL + N_HALF + N_QUARTER, 7, 5, 4, 3, 3, 2, 1]
LAST_SLOT = {1: (3, 3, 96, 128), 2: (2, 4, 64, 128), 3: (3, 3, 0, 96),
             5: (7, 0, 96, 128), 6: (2, 4, 0, 64), 7: (7, 0, 0, 96)}
ROTATE = [(P - a) % P for a in (LAST_SLOT[t][2] if t in LAST_SLOT else 0 for t in range(T))]
GATHERS = [SLOTS[t] - (t in LAST_SLOT and LAST_SLOT[t][0] != t) for t in range(T)]
FIRST = [sum(GATHERS[:t]) for t in range(T + 1)]
LIMIT = [2.0 * N] * CLS
LIMIT[FULL], LIMIT[FULL + 1], LIMIT[FULL + HALF] = 3 * P // 4, P // 2, P // 4
for _t in range(1, T):
    LIMIT[SLOTS[_t]] = min(LIMIT[SLOTS[_t]], _t * P)
    if _t in LAST_SLOT:
        _a, _b = LAST_SLOT[_t][2:]
        LIMIT[SLOTS[_t] - 1] = min(LIMIT[SLOTS[_t] - 1], _t * P + _b - _a)

V0 = 32
V1 = 8
NV = V0 + (T - 1) * V1
ORDER = list(range(2, T)) + [1]
GROUP = {}
_at = 0
for _t in ORDER:
    GROUP[_t] = _at
    _at += SLOTS[_t]
GROUP[0] = GROUP[1] + 8
NG = GROUP[0] + S
EARLY, LATE = [[1, 2], [3]], [4, 5, 6, 7]
LAST = [[0], [1, 2, 3], [5, 6, 7], [4]]
GATHER_ORDER = [0, 1, 2, 3, 5, 6, 7, 4]


def sort_groups(n):
    return [(0, 1, 1), (4, 8, 2), (1, 4, 3)] if isinstance(n, int) and n == 0 else [(0, 4, 2), (4, 8, 3)]


SPARE = 5
NF = N_HALF + N_QUARTER
FOLD = NV


def column(t, k):
    return V0 + V1 * (t - 1) + k


def scalar_mask(n):
    if isinstance(n, int) and n < 4:
        return [[], [0, 1, 2, 3], [2, 3], [3]][n]
    return [3]


def signs_before(n):
    if isinstance(n, int) and n < 4:
        return sum(len(scalar_mask(m)) for m in range(n))
    return signs_before(3) + len(scalar_mask(3)) + (n - 4) * len(scalar_mask(n))


CONST = {}
_at = 0
for _name, _w in (("pack", PK), ("before", P), ("ident", P), ("base", G), ("classes", CLS),
                  ("limit", CLS), ("bit", BITS), ("power", BITS), ("offset", B), ("node", T), ("minus_node", T)):
    CONST[_name] = (_at, _at + _w)
    _at += _w
NCONST = _at


def constants():
    c = np.zeros((P, NCONST), np.float32)
    p = np.arange(P)

    def put(name, a):
        c[:, CONST[name][0]:CONST[name][1]] = a

    pack = np.zeros((P, PK), np.float32)
    pack[p, p // BITS] = 2.0 ** (p % BITS)
    pack[:, GB] = 1.0
    put("pack", pack)
    put("before", p[:, None] < p[None, :])
    put("ident", p[:, None] == p[None, :])
    put("base", (G - np.arange(G)) * 2.0 ** BITS)
    put("classes", np.arange(CLS))
    put("limit", np.array(LIMIT))
    put("bit", np.arange(BITS))
    put("power", 2.0 ** np.arange(BITS))
    put("offset", np.arange(B) * TABLE)
    node = np.stack([P * t + (p + ROTATE[t]) % P for t in range(T)], axis=1)
    put("node", node)
    put("minus_node", -node)
    return c


def gnn_kernel(nc, x, x_t, table, adj_t, w, bias, const, out):
    with ExitStack() as ctx:
        def sb(name, shape, dt):
            return ctx.enter_context(nc.sbuf_tensor(name, shape, dt))

        def bank(name):
            return ctx.enter_context(nc.psum_tensor(name, [P, HN], F32))

        def sem(name):
            return ctx.enter_context(nc.semaphore(name))

        cst = sb("cst", [P, NCONST], F32)
        count_i = sb("count_i", [P, N], I32)
        pack = sb("pack", [P, PK], BF16)
        before = sb("before", [P, P], BF16)
        ident = sb("ident", [P, P], F16)
        base = sb("base", [P, G], BF16)
        count = sb("count", [P, N], F16)
        power = sb("power", [P, BITS], I32)
        ones = sb("ones", [P, P], BF16)
        ones_row = sb("ones_row", [1, P], F32)
        eps = sb("eps", [P, 1], F32)
        w_self = sb("w_self", [P, C], F32)
        w_agg = sb("w_agg", [P, C], F32)
        bias_row = sb("bias_row", [1, 4 * C], F32)

        raw = sb("raw", [P, T, N], I32)
        mask = sb("mask", [P, T, N], BF16)
        bits = sb("bits", [P, T, T, PK], BF16)
        high = sb("high", [P, T, G], BF16)
        degree = sb("degree", [P, T], F32)
        cls = sb("cls", [P, T], F32)
        same = sb("same", [P, T, CLS], BF16)
        above = sb("above", [P, T, CLS], BF16)
        picked = sb("picked", [P, T, CLS], F32)
        rank = sb("rank", [P, T], F32)
        rank16 = sb("rank16", [P, T], F16)
        rank_row = sb("rank_row", [P, 2, N], F16)
        low = sb("low", [P, B], F32)
        distance = sb("distance", [P, 2, N], F16)
        n_above = sb("n_above", [P, CLS], F32)
        broken = sb("broken", [P, CLS], F32)
        n_broken = sb("n_broken", [P, 1], F32)
        spare_flag = sb("spare_flag", [P, B], I32)
        floor = sb("floor", [P, B, T], F32)
        perm = sb("perm", [P, T, N], BF16)
        perm_t = sb("perm_t", [P, 2, T, N], BF16)
        keys = sb("keys", [P, T, G], F32)
        keys_left = sb("keys_left", [P, G], F32)
        tops = sb("tops", [P, GROUP[0] + V0], F32)
        tops_i = sb("tops_i", [P, NG], I32)
        tops_8 = sb("tops_8", [P, NG], I32)
        numbered = sb("numbered", [P, NG, BITS], F32)
        set_bits = sb("set_bits", [P, NG, BITS], I32)
        found = sb("found", [P, NG, BITS], F32)
        near = sb("near", [P, NV + NF], F32)
        index = sb("index", [P, 2, NV + NF], U32)
        rows = sb("rows", [P, FIRST[T], C], F32)
        head = sb("head", [P, 7, C], F32)
        agg = sb("agg", [P, T, C], F32)
        rest = sb("rest", [P, T, C], F32)
        part = sb("part", [P, 3, T, C], BF16)
        agg_t = sb("agg_t", [P, N], F32)
        x_in = sb("x_in", [P, T, C], F32)
        xt_in = sb("xt_in", [P, N], F32)
        z = sb("z", [P, T, C], F32)
        stats = sb("stats", [P, T, 6], F32)
        mean_var = sb("mean_var", [P, T, 2], F32)
        std = sb("std", [P, T], F32)
        inv_std = sb("inv_std", [P, T], F32)
        shift = sb("shift", [P, T], F32)
        y = sb("y", [P, T, C], F32)
        sp_keys = sb("sp_keys", [P, G], F32)
        sp_index = sb("sp_index", [P, V0], U32)
        sp_rows = sb("sp_rows", [P, SPARE, C], F32)
        sp_agg = sb("sp_agg", [P, 2, T, C], F32)

        banks = [bank(f"bank{i}") for i in range(8)]
        PER = [3, 3, 2]

        def bits_ps(i):
            return banks[i][:, 0:PER[i] * T * PK].rearrange("p (t j k) -> p t j k", t=PER[i], k=PK)

        rank_ps = banks[3][:, 0:T * CLS].rearrange("p (t d) -> p t d", t=T)
        above_ps = banks[3][:, T * CLS:(T + 1) * CLS]
        aggt_ps = (banks[6], banks[3])
        out_ps = (banks[7], banks[2])

        s_const = sem("constants_loaded")
        s_count = sem("count_made")
        s_weights = sem("weights_loaded")
        s_ready = sem("constants_made")
        s_raw = [sem(f"raw_loaded_{q}") for q in range(4)]
        s_mask = [sem(f"mask_made_{q}") for q in range(4)]
        s_sign = sem("signs_made")
        s_packed = sem("bits_packed")
        s_bits = sem("bits_copied")
        s_high = sem("high_made")
        s_class = sem("classes_made")
        s_ranked = sem("rank_sums_made")
        s_rank = sem("rank_made")
        s_above = sem("above_kept")
        s_row_ps = sem("rank_row_made")
        s_row = sem("rank_row_copied")
        s_perm = sem("perm_made")
        s_sorted = sem("keys_sorted")
        s_keys = sem("keys_copied")
        s_extract = sem("keys_used")
        s_index = sem("index_made")
        s_rows = [sem(f"rows_gathered_{t}") for t in range(T)]
        s_reduced = sem("rows_reduced")
        s_free = [sem(f"rows_free_{t}") for t in range(T)]
        s_agg = sem("agg_made")
        s_hi = sem("hi_made")
        s_rest = sem("rest_made")
        s_mid = sem("mid_made")
        s_lo = sem("lo_made")
        s_permt = sem("perm_t_made")
        s_permt_late = sem("perm_t_of_the_last_two_made")
        s_distance = sem("distance_made")
        s_turned = sem("agg_turned")
        s_aggt = sem("agg_t_copied")
        s_x = sem("x_loaded")
        s_xt = sem("x_t_loaded")
        s_self = sem("x_t_multiplied")
        s_lin = sem("linear_made")
        s_z = sem("z_made")
        s_var = sem("variance_made")
        s_std = sem("std_made")
        s_inv = sem("inverse_std_made")
        s_y = sem("y_made")
        s_y_last = sem("last_half_of_y_made")
        s_out = [sem(f"out_stored_{h}") for h in range(2)]
        s_spidx = sem("spare_index_made")
        s_sprows = sem("spare_rows_gathered")
        s_spfree = sem("spare_rows_free")
        s_step = sem("vector_steps")
        s_spare_step = sem("vector_steps_of_the_spare_path")

        def wait(eng, s, value):
            if not isinstance(value, int) or value > 0:
                eng.wait_ge(s, value)

        block = ctx.enter_context(nc.Block())


        @block.sync
        def _(sp):
            def load_adj(n):
                for q in range(4):
                    wait(sp, s_mask[q], n)
                    sp.dma_start(raw[:, 2 * q:2 * q + 2, :],
                                 adj_t[bass.ds(n, 1), 2 * q * P:(2 * q + 2) * P, :]
                                 .rearrange("a (j p) i -> p (a j) i", p=P)).then_inc(s_raw[q], 16)

            def load_x(n):
                wait(sp, s_self, 2 * n)
                sp.dma_start(xt_in[:, :], x_t[bass.ds(n, 1), :, :].rearrange("a c i -> c (a i)")).then_inc(s_xt, 16)
                wait(sp, s_z, 2 * n)
                sp.dma_start(x_in[:, :, :], x[bass.ds(n, 1), :, :].rearrange("a (t p) c -> p (a t) c", p=P)).then_inc(s_x, 16)

            load_adj(0)
            load_adj(1)
            sp.dma_start(w_self[:, :], w[0:C, :]).then_inc(s_weights, 16)
            sp.dma_start(w_agg[:, :], w[C:2 * C, :]).then_inc(s_weights, 16)
            sp.dma_start(bias_row[:, :], bias).then_inc(s_weights, 16)
            load_adj(2)
            load_x(0)
            load_adj(3)
            with sp.Fori(1, B - 3) as n:
                load_adj(n + 3)
                load_x(n)
            for n in range(B - 3, B):
                load_x(n)
            sp.wait_ge(s_y_last, 1)
            sp.dma_start(out[B - 1:B, HN:N, :].rearrange("a (t p) c -> p (a t) c", p=P), y[:, 4:8, :]).then_inc(s_out[1], 16)
            sp.wait_ge(s_out[1], 16 * B)

        @block.gpsimd
        def _(pool):
            def gather(dst, idx, done):
                pool.indirect_dma_start(dst, None, table, bass.IndirectOffsetOnAxis(ap=idx, axis=0)).then_inc(done, 16)

            def spare(n):
                flag = pool.value_load(spare_flag[0:1, bass.ds(n, 1)], min_val=0, max_val=CLS)
                with pool.If(flag > 0):
                    with pool.Fori(0, T):
                        pool.wait_ge(s_spidx, 1)
                        pool.sem_clear(s_spidx)
                        for k in range(S):
                            if k % SPARE == 0 and k > 0:
                                pool.wait_ge(s_spfree, 1)
                                pool.sem_clear(s_spfree)
                            gather(sp_rows[:, k % SPARE, :], sp_index[:, k:k + 1], s_sprows)

            def gathers(n, side):
                first = isinstance(n, int) and n == 0
                pool.wait_ge(s_index, 1 if first else 3 * n + 3)
                spare(n)
                for t in GATHER_ORDER:
                    if not isinstance(n, int) or n > 0:
                        pool.wait_ge(s_free[t], 1)
                        pool.sem_clear(s_free[t])
                    if first and t == 1:
                        pool.wait_ge(s_index, 3)
                    columns = (list(range(FULL)) + list(range(FOLD, FOLD + NF)) if t == 0 else
                               [column(t, k) for k in range(GATHERS[t])])
                    for k, col in enumerate(columns):
                        if first and t == 0 and k == FULL:
                            pool.wait_ge(s_index, 2)
                        gather(rows[:, FIRST[t] + k, :], index[:, side, col:col + 1], s_rows[t])

            for t in range(T):
                for a, b, node in ((0, P - ROTATE[t], P * t + ROTATE[t]), (P - ROTATE[t], P, P * t)):
                    if a < b:
                        ins = pool.iota(count_i[:, P * t + a:P * t + b], [[1, b - a]], base=node, channel_multiplier=0)
            ins.then_inc(s_count, 1)
            gathers(0, 0)
            gathers(1, 1)
            with pool.Fori(1, B // 2) as pair:
                gathers(2 * pair, 0)
                gathers(2 * pair + 1, 1)

        @block.tensor
        def _(pe):
            def pack_bits(n):
                if isinstance(n, int) and n == 0:
                    pe.wait_ge(s_ready, 2)
                wait(pe, s_row, n)
                wait(pe, s_class, n)
                wait(pe, s_bits, 3 * n)
                wait(pe, s_z, 2 * (n - 3))
                for j in range(T):
                    if j % 2 == 0:
                        pe.wait_ge(s_mask[j // 2], n + 1)
                    for t in range(T):
                        last = nc.tensor.matmul(bits_ps(t // 3)[:, t % 3, j, :], mask[:, j, t * P:(t + 1) * P],
                                                pack[:, :], start=True, stop=True)
                last.then_inc(s_packed, 1)

            def rank_nodes(n):
                pe.wait_ge(s_class, n + 1)
                wait(pe, s_above, n)
                wait(pe, s_rank, n)
                wait(pe, s_aggt, 2 * (n - 3))
                nc.tensor.matmul(rank_ps[:, :, :], before[:, :], same[:, :, :], start=True, stop=False)
                for t in range(T - 1):
                    nc.tensor.matmul(rank_ps[:, t + 1:, :], ones[:, :],
                                     same[:, t:t + 1, :].to_broadcast([P, T - 1 - t, CLS]), start=False, stop=False)
                for t in range(T):
                    nc.tensor.matmul(rank_ps[:, :, :], ones[:, :], above[:, t:t + 1, :].to_broadcast([P, T, CLS]),
                                     start=False, stop=(t == T - 1))
                for t in range(T):
                    last = nc.tensor.matmul(above_ps, ones[:, :], above[:, t, :], start=(t == 0), stop=(t == T - 1))
                last.then_inc(s_ranked, 1)

            def spread_rank(n):
                pe.wait_ge(s_rank, n + 1)
                pe.wait_ge(s_bits, 3 * (n + 1))
                for t in range(T):
                    last = nc.tensor.matmul(banks[t // 4][:, (t % 4) * P:(t % 4 + 1) * P],
                                            rank16[:, t:t + 1].to_broadcast([P, P]), ident[:, :], start=True, stop=True)
                last.then_inc(s_row_ps, 1)

            def sort_keys(n):
                wait(pe, s_keys, 3 * n)
                pe.wait_ge(s_high, n + 1)
                pe.wait_ge(s_perm, 2 * n + 1)
                counted = 0
                for g, (a, b, upto) in enumerate(sort_groups(n)):
                    if b > 1:
                        pe.wait_ge(s_perm, 2 * n + 2)
                    if g == 2:
                        pe.wait_ge(s_keys, 3 * n + 1)
                    for r in range(a, b):
                        dst = banks[4 + r // 4][:, (r % 4) * G:(r % 4 + 1) * G]
                        for t in range(T):
                            weights = perm[:, t, r * P:(r + 1) * P]
                            nc.tensor.matmul(dst, weights, bits[:, t, :, 0:GB], start=(t == 0), stop=False)
                            last = nc.tensor.matmul(dst, weights, high[:, t, :], start=False, stop=(t == T - 1))
                    last.then_inc(s_sorted, upto - counted)
                    counted = upto

            def turn_agg(n, side, h, newest, tiles=range(T), group=0, complete=True):
                if tiles[0] == 0:
                    if h == 0:
                        if isinstance(n, int) and n >= B - 2:
                            pe.wait_ge(s_permt_late, n + 1 - (B - 2))
                        else:
                            pe.wait_ge(s_permt, T * (n + 1))
                        wait(pe, s_aggt, 2 * n - 1)
                    else:
                        wait(pe, s_aggt, 2 * n)
                        pe.wait_ge(s_rank, newest + 1)
                        pe.wait_ge(s_above, newest + 1)
                if h == 0:
                    pe.wait_ge(s_hi, n + 1 + group)
                    pe.wait_ge(s_mid, n + 1 + group)
                    pe.wait_ge(s_lo, n + 1 + group)
                for r in tiles:
                    turned = perm_t[:, side, r, h * HN:(h + 1) * HN]
                    for k in range(3):
                        last = nc.tensor.matmul(aggt_ps[h][:, :], part[:, k, r, :], turned,
                                                start=(r == 0 and k == 0), stop=(complete and r == tiles[-1] and k == 2))
                if complete:
                    last.then_inc(s_turned, 1)

            def out_tiles(h):
                return [(t, out_ps[h][:, (t % 4) * C:(t % 4 + 1) * C]) for t in range(4 * h, 4 * h + 4)]

            def linear_self(n, h, newest):
                pe.wait_ge(s_xt, 16 * (n + 1))
                wait(pe, s_z, 2 * n + h - 1)
                if h == 1:
                    pe.wait_ge(s_bits, 3 * (newest + 1))
                nc.tensor.matmul(out_ps[h][:, :], ones_row[:, :], bias_row[:, :], start=True, stop=False)
                for t, dst in out_tiles(h):
                    last = nc.tensor.matmul(dst, xt_in[:, t * P:(t + 1) * P], w_self[:, :], start=False, stop=False)
                last.then_inc(s_self, 1)

            def linear_agg(n, h):
                pe.wait_ge(s_aggt, 2 * n + h + 1)
                for t, dst in out_tiles(h):
                    last = nc.tensor.matmul(dst, agg_t[:, t * P:(t + 1) * P], w_agg[:, :], start=False,
                                            stop=(t % 4 == 3))
                last.then_inc(s_lin, 1)

            def keep_warm(products, bank):
                for _ in range(products):
                    nc.tensor.matmul(bank[:, :], ident[:, :], count[:, 0:HN], start=True, stop=True)

            def step(n, side, first=False, late=False):
                newest = B - 1 if late else n + 2
                if not late:
                    pack_bits(n + 2)
                if not first:
                    for h in range(2):
                        linear_self(n - 1, h, newest)
                if not late:
                    rank_nodes(n + 2)
                if not first:
                    for h in range(2):
                        turn_agg(n - 1, 1 - side, h, newest)
                if not late:
                    spread_rank(n + 2)
                if not first:
                    for h in range(2):
                        linear_agg(n - 1, h)
                if first:
                    keep_warm(5, banks[7])
                if not late:
                    sort_keys(n + 2)

            pack_bits(0)
            keep_warm(5, banks[7])
            rank_nodes(0)
            keep_warm(4, banks[7])
            spread_rank(0)
            keep_warm(1, banks[7])
            sort_keys(0)
            pack_bits(1)
            rank_nodes(1)
            spread_rank(1)
            keep_warm(6, banks[7])
            sort_keys(1)
            step(0, 0, first=True)
            pe.wait_ge(s_weights, 48)
            step(1, 1)
            with pe.Fori(1, B // 2 - 1) as pair:
                for side in range(2):
                    step(2 * pair + side, side)
            step(B - 2, 0, late=True)
            step(B - 1, 1, late=True)
            for h in range(2):
                linear_self(B - 1, h, B - 1)
            pe.wait_ge(s_keys, 3 * B)
            keep_warm(3, banks[4])
            for g, tiles in enumerate(LAST):
                for h in range(2):
                    turn_agg(B - 1, 1, h, B - 1, tiles, g, g == len(LAST) - 1)
            for h in range(2):
                linear_agg(B - 1, h)

        @block.scalar
        def _(act):
            def copy_bits(n):
                act.wait_ge(s_packed, n + 1)
                wait(act, s_sorted, 3 * n)
                for i in range(3):
                    nc.scalar.copy(bits[:, 3 * i:3 * i + PER[i], :, :], bits_ps(i)).then_inc(s_bits, 1)

            def copy_ranks(n, side):
                act.wait_ge(s_row_ps, n + 1)
                wait(act, s_permt, T * (n - 1))
                for h in range(2):
                    ins = nc.scalar.copy(rank_row[:, side, h * HN:(h + 1) * HN], banks[h][:, :])
                ins.then_inc(s_row, 1)

            def copy_keys(n, groups=None):
                wait(act, s_extract, n)
                groups = groups or sort_groups(n)
                counted = 0 if groups[0][0] == 0 else 1
                for a, b, upto in groups:
                    act.wait_ge(s_sorted, 3 * n + upto)
                    nc.scalar.copy(keys[:, a:b, :].rearrange("p t g -> p (t g)"),
                                   banks[4 + a // 4][:, a % 4 * G:(a % 4 + b - a) * G]).then_inc(s_keys, upto - counted)
                    counted = upto

            def make_mask(n, quarters=None):
                quarters = quarters or scalar_mask(n)
                signs = signs_before(n)
                for q in quarters:
                    act.wait_ge(s_raw[q], 16 * (n + 1))
                    act.wait_ge(s_packed, n)
                    quarter = mask[:, 2 * q:2 * q + 2, :]
                    nc.scalar.activation(quarter, raw[:, 2 * q:2 * q + 2, :], ACT.Sign).then_inc(s_sign, 1)
                    act.wait_ge(s_sign, signs + scalar_mask(n).index(q) + 1)
                    nc.scalar.activation(quarter, quarter, ACT.Square).then_inc(s_mask[q], 1)

            def high_part(n, a=0, b=T, group=0):
                act.wait_ge(s_agg, n + 1 + group)
                wait(act, s_turned, 2 * n)
                nc.scalar.copy(part[:, 0, a:b, :], agg[:, a:b, :]).then_inc(s_hi, 1)

            def middle_part(n, a=0, b=T, group=0):
                act.wait_ge(s_rest, n + 1 + group)
                nc.scalar.copy(part[:, 1, a:b, :], rest[:, a:b, :]).then_inc(s_mid, 1)

            def transpose_perm(n, side, tiles):
                act.wait_ge(s_row, n + 1)
                wait(act, s_turned, 2 * (n - 1))
                for t in tiles:
                    wait(act, s_permt, T * n + t - 1)
                    nc.scalar.activation(distance[:, t % 2, :], rank_row[:, side, :],
                                         ACT.Abs, bias=cst[:, CONST["minus_node"][0] + t:CONST["minus_node"][0] + t + 1]
                                         ).then_inc(s_distance, 1)
                    act.wait_ge(s_distance, T * n + t + 1)
                    nc.scalar.activation(perm_t[:, side, t, :], distance[:, t % 2, :],
                                         ACT.Relu, bias=1.0, scale=-1.0).then_inc(s_permt, 1)

            def copy_turned(n, h):
                act.wait_ge(s_turned, 2 * n + h + 1)
                wait(act, s_lin, 2 * (n - 1) + h + 1)
                nc.scalar.copy(agg_t[:, h * HN:(h + 1) * HN], aggt_ps[h][:, :]).then_inc(s_aggt, 1)

            def root(n, h):
                act.wait_ge(s_var, 2 * n + h + 1)
                nc.scalar.activation(std[:, 4 * h:4 * h + 4], mean_var[:, 4 * h:4 * h + 4, 1], ACT.Sqrt,
                                     bias=eps[:, 0:1]).then_inc(s_std, 1)

            def normalise(n, h):
                act.wait_ge(s_inv, 2 * n + h + 1)
                wait(act, s_out[h], 16 * n)
                for t in range(4 * h, 4 * h + 4):
                    ins = nc.scalar.activation(y[:, t, :], z[:, t, :], ACT.Identity, bias=shift[:, t:t + 1],
                                               scale=inv_std[:, t:t + 1])
                ins.then_inc(s_y, 1)
                act.wait_ge(s_y, 2 * n + h + 1)
                act.dma_start(out[bass.ds(n, 1), h * HN:(h + 1) * HN, :].rearrange("a (t p) c -> p (a t) c", p=P),
                              y[:, 4 * h:4 * h + 4, :]).then_inc(s_out[h], 16)

            def step(n, side, first=False, late=False):
                early = isinstance(n, int) and n < 2
                if not (early or late):
                    make_mask(n + 2)
                if not first:
                    high_part(n - 1)
                if not late:
                    copy_bits(n + 2)
                if not first:
                    middle_part(n - 1)
                if not (isinstance(n, int) and n < 2):
                    for h in range(2):
                        normalise(n - 2, h)
                if not late:
                    transpose_perm(n, side, range(0, 3))
                if not first:
                    copy_turned(n - 1, 0)
                if not late:
                    transpose_perm(n, side, range(3, 5))
                if not first:
                    copy_turned(n - 1, 1)
                if not late:
                    transpose_perm(n, side, range(5, T))
                    copy_ranks(n + 2, side)
                if not first:
                    for h in range(2):
                        root(n - 1, h)
                if first:
                    make_mask(3)
                if not late:
                    copy_keys(n + 2)

            act.dma_start(cst[:, :], const).then_inc(s_const, 16)
            act.wait_ge(s_const, 16)
            nc.scalar.copy(ident[:, :], cst[:, CONST["ident"][0]:CONST["ident"][1]]).then_inc(s_ready, 1)
            copy_bits(0)
            make_mask(1, [0, 1])
            copy_keys(0, sort_groups(0)[:1])
            copy_ranks(0, 0)
            make_mask(1, [2, 3])
            copy_keys(0, sort_groups(0)[1:])
            copy_bits(1)
            copy_ranks(1, 1)
            make_mask(2)
            copy_keys(1)
            step(0, 0, first=True)
            step(1, 1)
            with act.Fori(1, B // 2 - 1) as pair:
                for side in range(2):
                    step(2 * pair + side, side)
            step(B - 2, 0, late=True)
            step(B - 1, 1, late=True)
            for g, tiles in enumerate(LAST):
                high_part(B - 1, tiles[0], tiles[-1] + 1, g)
                middle_part(B - 1, tiles[0], tiles[-1] + 1, g)
                if g in (0, len(LAST) - 1):
                    normalise(B - 2, 0 if g == 0 else 1)
            for h in range(2):
                copy_turned(B - 1, h)
            for h in range(2):
                root(B - 1, h)
            normalise(B - 1, 0)
            act.wait_ge(s_out[0], 16 * B)

        @block.vector
        def _(v):
            def const_of(name):
                return cst[:, CONST[name][0]:CONST[name][1]]

            class Steps:

                def __init__(self, semaphore=s_step):
                    self.done, self.semaphore = 0, semaphore

                def __call__(self, ins):
                    ins.then_inc(self.semaphore, 1)
                    self.done += 1
                    return self.done

                def settle(self, upto=None):
                    v.wait_ge(self.semaphore, self.done if upto is None else upto)

                def end(self):
                    self.settle()
                    v.sem_clear(self.semaphore)

            v.wait_ge(s_const, 16)
            setup = Steps()
            for dst, name in ((pack, "pack"), (before, "before"), (base, "base"), (power, "power")):
                setup(v.tensor_copy(dst[:, :], const_of(name)))
            setup(v.memset(ones[:, :], 1.0))
            setup(v.memset(ones_row[:, :], 1.0))
            setup(v.memset(eps[:, :], EPS))
            v.wait_ge(s_count, 1)
            setup(v.tensor_copy(count[:, :], count_i[:, :]))
            setup.end()
            v.sem_inc(s_ready, 1)

            def reduce_slots(dst, src):
                return v.tensor_reduce(dst, src.rearrange("p k c -> p c k"), AX.X, ALU.max)

            def top_eights(step, src, left, dst, rounds, others=()):
                others = list(others)
                for r in range(rounds):
                    for half in range(1 if r == rounds - 1 else 2):
                        if half == 0:
                            made = step(v.max(out=dst[:, 8 * r:8 * r + 8], in_=src))
                        else:
                            made = step(v.match_replace(out=left, in_to_replace=dst[:, 8 * r:8 * r + 8], in_values=src,
                                                        imm_value=0.0))
                            src = left
                        if others:
                            step.settle(made - 1)
                            step(others.pop(0)())
                        step.settle(made)
                assert not others

            def expand(step, a, b):
                m = b - a
                step.settle()
                step(v.tensor_copy(tops_i[:, a:b], tops[:, a:b]))
                step.settle()
                step(v.tensor_scalar(tops_8[:, a:b], tops_i[:, a:b], BITS - 3, (2 * G - 1) * BITS,
                                     ALU.logical_shift_right, ALU.bitwise_and))
                step(v.tensor_tensor(set_bits[:, a:b, :], tops_i[:, a:b].unsqueeze(2).to_broadcast([P, m, BITS]),
                                     power[:, :].unsqueeze(1).to_broadcast([P, m, BITS]), ALU.bitwise_and))
                step.settle(step.done - 1)
                step(v.tensor_tensor(numbered[:, a:b, :], tops_8[:, a:b].unsqueeze(2).to_broadcast([P, m, BITS]),
                                     const_of("bit").unsqueeze(1).to_broadcast([P, m, BITS]), ALU.subtract))
                step.settle()
                step(v.scalar_tensor_tensor(out=found[:, a:b, :], in0=set_bits[:, a:b, :], scalar=0.0,
                                            in1=numbered[:, a:b, :], op0=ALU.not_equal, op1=ALU.mult))
                step.settle()

            flat = found[:, :, :].rearrange("p v k -> p (v k)")
            flat_0 = flat[:, GROUP[0] * BITS:NG * BITS]

            spare_tiles = v.alloc_register("tiles_through_the_spare_path")
            v.reg_mov(spare_tiles, 0)
            flags = [v.alloc_register(f"spare_flag_{side}") for side in range(2)]

            def load_flag(n, side):
                v.reg_mov(flags[side], v.value_load(spare_flag[0:1, bass.ds(n, 1)], min_val=0, max_val=CLS))

            def broken_limit(side):
                return v.snap(flags[side], min_val=0, max_val=CLS) > 0

            def spare(n, side):
                with v.If(broken_limit(side)):
                    with v.Fori(0, T) as t:
                        before = v.snap(spare_tiles, min_val=0, max_val=B * T - 1)
                        v.reg_add(spare_tiles, spare_tiles, 1)
                        step = Steps(s_spare_step)
                        step(v.tensor_copy(sp_keys[:, :], keys[:, bass.ds(t, 1), :].rearrange("p a g -> p (a g)")))
                        step.settle()
                        top_eights(step, sp_keys[:, :], keys_left[:, :], tops[:, GROUP[0]:], V0 // 8)
                        expand(step, GROUP[0], NG)
                        top_eights(step, flat_0, flat_0, near, V0 // 8)
                        step(v.tensor_scalar(sp_index[:, :], near[:, 0:V0],
                                             const_of("offset")[:, bass.ds(n, 1)], None, ALU.add))
                        step.end()
                        v.sem_inc(s_spidx, 1)
                        step = Steps(s_spare_step)
                        for i in range(S // SPARE):
                            v.wait_ge(s_sprows, before * (16 * S) + 16 * SPARE * (i + 1))
                            step(reduce_slots(head[:, i, :], sp_rows[:, :, :]))
                            step.settle()
                            if i < S // SPARE - 1:
                                v.sem_inc(s_spfree, 1)
                        step(v.tensor_reduce(sp_agg[:, side, bass.ds(t, 1), :].rearrange("p a c -> p (a c)"),
                                             head[:, 0:S // SPARE, :].rearrange("p k c -> p c k"), AX.X, ALU.max))
                        step.end()

            def make_mask(n):
                wait(v, s_packed, n)
                for q in range(4):
                    if q in scalar_mask(n):
                        continue
                    v.wait_ge(s_raw[q], 16 * (n + 1))
                    v.tensor_scalar(mask[:, 2 * q:2 * q + 2, :], raw[:, 2 * q:2 * q + 2, :], 0.0, None,
                                    ALU.not_equal).then_inc(s_mask[q], 1)

            def classify(step, n):
                v.wait_ge(s_bits, 3 * (n + 1))
                step(v.tensor_reduce(degree[:, :], bits[:, :, :, GB], AX.X, ALU.add))
                step.settle()
                step(v.tensor_scalar(cls[:, :], degree[:, :], float(CLS - 1), None, ALU.min))
                step.settle()
                a = cls[:, :].unsqueeze(2).to_broadcast([P, T, CLS])
                b = const_of("classes").unsqueeze(1).to_broadcast([P, T, CLS])
                step(v.tensor_tensor(same[:, :, :], a, b, ALU.is_equal))
                v.tensor_tensor(above[:, :, :], a, b, ALU.is_gt).then_inc(s_class, 1)
                wait(v, s_sorted, 3 * n)
                v.scalar_tensor_tensor(out=high[:, :, :].rearrange("p t (j k) -> p t j k", k=GB),
                                       in0=bits[:, :, :, 0:GB], scalar=0.0,
                                       in1=base[:, :].rearrange("p (j k) -> p j k", k=GB).unsqueeze(1).to_broadcast([P, T, T, GB]),
                                       op0=ALU.is_gt, op1=ALU.mult).then_inc(s_high, 1)

            def make_perm(step, n):
                v.wait_ge(s_ranked, n + 1)
                step(v.tensor_tensor(picked[:, :, :], rank_ps[:, :, :], same[:, :, :], ALU.mult))
                v.tensor_copy(n_above[:, :], above_ps).then_inc(s_above, 1)
                step.settle()
                step(v.tensor_reduce(rank[:, :], picked[:, :, :], AX.X, ALU.add))
                step.settle()
                v.tensor_copy(rank16[:, :], rank[:, :]).then_inc(s_rank, 1)
                pieces = ((0, P), (P, N)) if isinstance(n, int) and n == 0 else ((0, N),)
                for a, b in pieces:
                    for t in range(T):
                        ins = v.tensor_scalar(perm[:, t, a:b], count[:, a:b], rank[:, t:t + 1], None, ALU.is_equal)
                    ins.then_inc(s_perm, 2 // len(pieces))

            def check_limits(step, n):
                v.wait_ge(s_above, n + 1)
                a = step(v.tensor_tensor(broken[:, :], n_above[:, :], const_of("limit"), ALU.is_gt))
                step(v.tensor_scalar(floor[:, bass.ds(n, 1), :].rearrange("p a t -> p (a t)"), const_of("node"),
                                     n_above[:, S:S + 1], -BIG, ALU.is_lt, ALU.mult))
                step.settle(a)
                step(v.tensor_reduce(n_broken[:, :], broken[:, :], AX.X, ALU.add))
                step.settle()
                step(v.tensor_copy(spare_flag[:, bass.ds(n, 1)], n_broken[:, :]))
                step(v.tensor_scalar(low[:, bass.ds(n, 1)], n_broken[:, :], 0.0, -BIG, ALU.is_gt, ALU.mult))

            groups_of = [lambda t=t: v.max(out=tops[:, GROUP[t]:GROUP[t] + 8], in_=keys[:, t, :]) for t in ORDER]
            nodes_of = [lambda t=t: v.max(out=near[:, V0 + V1 * (t - 1):V0 + V1 * t],
                                          in_=flat[:, BITS * GROUP[t]:BITS * (GROUP[t] + SLOTS[t])])
                        for t in range(1, T)]

            def head_groups(step, others):
                top_eights(step, keys[:, 0, :], keys_left[:, :], tops[:, GROUP[0]:], V0 // 8, others)

            def head_nodes(step, others):
                top_eights(step, flat_0, flat_0, near, V0 // 8, others)

            def fold(step):
                a, h = FULL, P // 2
                step(v.tensor_copy(near[0:h, FOLD:FOLD + N_HALF], near[0:h, a:a + HALF:2]))
                step(v.tensor_copy(near[h:P, FOLD:FOLD + N_HALF], near[0:h, a + 1:a + HALF:2]))
                a, h = FULL + HALF, P // 4
                c0, c1 = FOLD + N_HALF, FOLD + NF
                for i, s in enumerate(QUADRANTS):
                    k = (QUARTER - i + 3) // 4
                    step(v.tensor_copy(near[s * h:(s + 1) * h, c0:c0 + k], near[0:h, a + i:a + QUARTER:4]))
                step(v.tensor_copy(near[THIRD, c1 - 1:c1], near[THIRD, FULL:FULL + 1]))

            def share(step):
                step.settle(step.done - 1)
                for t, (host, slot, a, b) in LAST_SLOT.items():
                    if host != t:
                        to, own = column(host, slot), column(t, SLOTS[t] - 1)
                        step(v.tensor_copy(near[a:b, to:to + 1], near[a:b, own:own + 1]))

            def to_index(n, side, a, b):
                return v.tensor_scalar(index[:, side, a:b], near[:, a:b], const_of("offset")[:, bass.ds(n, 1)], None, ALU.add)

            def best_groups(step, n):
                v.wait_ge(s_keys, 3 * (n + 1))
                check_limits(step, n)
                head_groups(step, groups_of)

            def make_index(step, n, side):
                head_nodes(step, nodes_of)
                fold(step)
                share(step)
                step.settle()
                to_index(n, side, 0, NV + NF).then_inc(s_index, 3)
                spare(n, side)
                v.sem_inc(s_extract, 1)

            def first_head_index(step):
                check_limits(step, 0)
                v.wait_ge(s_keys, 1)
                g = GROUP[0]
                step(v.max(out=tops[:, g:g + 8], in_=keys[:, 0, :]))
                expand(step, g, g + 8)
                step(v.max(out=near[:, 0:8], in_=flat_0[:, 0:8 * BITS]))
                step.settle()
                to_index(0, 0, 0, 8).then_inc(s_index, 1)
                head_groups(step, ())
                expand(step, g, NG)
                head_nodes(step, ())
                fold(step)
                step.settle()
                to_index(0, 0, FOLD, FOLD + NF).then_inc(s_index, 1)
                load_flag(0, 0)

            def other_groups(step):
                for work in groups_of:
                    step(work())
                    step.settle()

            def first_other_index(step):
                v.wait_ge(s_keys, 3)
                other_groups(step)
                expand(step, 0, GROUP[0])
                for work in nodes_of:
                    step(work())
                step.settle()
                share(step)
                step.settle()
                to_index(0, 0, V0, NV).then_inc(s_index, 1)
                spare(0, 0)
                v.sem_inc(s_extract, 1)

            def transpose_perm(n, side):
                v.wait_ge(s_row, n + 1)
                v.wait_ge(s_turned, 2 * (n - 1))
                for t in range(T):
                    ins = v.tensor_scalar(perm_t[:, side, t, :], rank_row[:, side, :],
                                          const_of("node")[:, t:t + 1], None, ALU.is_equal)
                ins.then_inc(s_permt_late, 1)

            def reduce_head(step, n):
                wait(v, s_lo, n)
                v.wait_ge(s_rows[0], 16 * SLOTS[0] * (n + 1))
                r0, r1, r2 = FULL, FULL + N_HALF, SLOTS[0]
                assert r2 - r1 == 3
                last = rows[:, r2 - 1, :]
                made = step(v.tensor_tensor(head[:, 3, :], rows[:, r1, :], rows[:, r1 + 1, :], ALU.max))
                step(reduce_slots(head[:, 0, :], rows[:, 0:r0, :]))
                step.settle(made)
                for others in (slice(0, THIRD.start), slice(THIRD.stop, P)):
                    step(v.tensor_tensor(head[others, 3, :], head[others, 3, :], last[others, :], ALU.max))
                made = step(reduce_slots(head[:, 1, :], rows[:, r0:r1, :]))
                step.settle(made - 1)
                step(v.tensor_tensor(agg[THIRD, 0, :], head[THIRD, 0, :], last[THIRD, :], ALU.max))
                for i in range(1, 4):
                    step(v.tensor_copy(head[0:32, 3 + i, :], head[32 * i:32 * i + 32, 3, :]))
                step.settle(made)
                step(v.tensor_copy(head[0:64, 2, :], head[64:128, 1, :]))
                step(v.tensor_copy(agg[96:128, 0, :], head[96:128, 0, :]))
                step.settle(step.done - 1)
                v.sem_inc(s_free[0], 1)
                step(reduce_slots(agg[32:64, 0, :], head[32:64, 0:3, :]))
                step(reduce_slots(agg[0:32, 0, :], head[0:32, :, :]))

            def reduce_tiles(step, n, tiles):
                made = {}
                for t in tiles:
                    v.wait_ge(s_rows[t], 16 * GATHERS[t] * (n + 1))
                    whole = SLOTS[t] - (t in LAST_SLOT)
                    src = rows[:, FIRST[t]:FIRST[t] + whole, :]
                    if whole > 1:
                        made[t] = step(reduce_slots(agg[:, t, :], src))
                    elif whole == 1:
                        made[t] = step(v.tensor_copy(agg[:, t, :], src[:, 0, :]))
                    else:
                        a, b = LAST_SLOT[t][2:]
                        step(v.tensor_copy(agg[a:b, t, :], rows[a:b, FIRST[t], :]))
                        step(v.memset(agg[b:P, t, :], 0.0))
                for t, (host, slot, a, b) in LAST_SLOT.items():
                    if max(t, host) in tiles and SLOTS[t] > 1:
                        step.settle(made.get(t))
                        step(v.tensor_tensor(agg[a:b, t, :], agg[a:b, t, :], rows[a:b, FIRST[host] + slot, :], ALU.max))

            def free_rows(step, tiles):
                step.settle()
                for t in tiles:
                    v.sem_inc(s_free[t], 1)

            def finish_agg(step, n, side, a=0, b=T):
                with v.If(broken_limit(side)):
                    step.settle()
                    spare_step = Steps(s_spare_step)
                    for t in range(a, b):
                        spare_step(v.tensor_scalar(agg[:, t, :], sp_agg[:, side, t, :], floor[:, bass.ds(n, 1), t], None,
                                                   ALU.max))
                    spare_step.end()
                    v.sem_inc(s_agg, 1)
                with v.Else():
                    step.settle()
                    v.sem_inc(s_agg, 1)

            def split_rest(n, a=0, b=T, group=0):
                v.wait_ge(s_hi, n + 1 + group)
                pieces = [(floor[:, bass.ds(n, 1), 0], 0, 1)] if a == 0 else []
                if b > 1:
                    pieces.append((low[:, bass.ds(n, 1)], max(a, 1), b))
                for scalar, i, j in pieces:
                    ins = v.scalar_tensor_tensor(out=rest[:, i:j, :], in0=agg[:, i:j, :], scalar=scalar,
                                                 in1=part[:, 0, i:j, :], op0=ALU.max, op1=ALU.subtract)
                ins.then_inc(s_rest, 1)

            def split_low(n, a=0, b=T, group=0):
                v.wait_ge(s_mid, n + 1 + group)
                v.tensor_tensor(part[:, 2, a:b, :], rest[:, a:b, :], part[:, 1, a:b, :], ALU.subtract).then_inc(s_lo, 1)

            def layer_norm(step, n, h):
                tiles = range(4 * h, 4 * h + 4)
                v.wait_ge(s_x, 16 * (n + 1))
                v.wait_ge(s_lin, 2 * n + h + 1)
                wait(v, s_y, 2 * (n - 1) + h + 1)
                v.scalar_tensor_tensor(out=z[:, 4 * h:4 * h + 4, :], in0=out_ps[h][:, :].rearrange("p (t c) -> p t c", c=C),
                                       scalar=0.0, in1=x_in[:, 4 * h:4 * h + 4, :],
                                       op0=ALU.max, op1=ALU.add).then_inc(s_z, 1)
                v.wait_ge(s_z, 2 * n + h + 1)
                for t in tiles:
                    step(v.bn_stats(stats[:, t, :], z[:, t, :]))
                step.settle()
                for t in tiles:
                    ins = v.bn_aggr(mean_var[:, t, :], stats[:, t, :])
                ins.then_inc(s_var, 1)

            def invert(step, n, halves):
                for h in halves:
                    v.wait_ge(s_std, 2 * n + h + 1)
                    step(v.reciprocal(inv_std[:, 4 * h:4 * h + 4], std[:, 4 * h:4 * h + 4]))
                step.settle()
                for h in halves:
                    v.scalar_tensor_tensor(out=shift[:, 4 * h:4 * h + 4], in0=mean_var[:, 4 * h:4 * h + 4, 0], scalar=-1.0,
                                           in1=inv_std[:, 4 * h:4 * h + 4], op0=ALU.mult, op1=ALU.mult).then_inc(s_inv, 1)

            def step_of(step, n, side, first=False, late=False, last=False):
                if not late:
                    make_mask(n + 2)
                if not first:
                    reduce_tiles(step, n - 1, LATE)
                    finish_agg(step, n - 1, 1 - side)
                    free_rows(step, [2] + LATE)
                if first:
                    reduce_head(step, n)
                if not last:
                    if not first:
                        best_groups(step, n + 1)
                    else:
                        v.wait_ge(s_keys, 3 * (n + 1) + 2)
                        check_limits(step, n + 1)
                        head_groups(step, ())
                        v.wait_ge(s_keys, 3 * (n + 2))
                        other_groups(step)
                        load_flag(n + 1, 1 - side)
                        expand(step, 0, NG)
                        make_index(step, n + 1, 1 - side)
                if not first:
                    split_rest(n - 1)
                if not late:
                    classify(step, n + 2)
                if not first:
                    split_low(n - 1)
                    if not last:
                        expand(step, 0, NG)
                if not late:
                    make_perm(step, n + 2)
                if not first:
                    if not last:
                        load_flag(n + 1, 1 - side)
                        make_index(step, n + 1, 1 - side)
                    reduce_head(step, n)
                if late:
                    transpose_perm(n, side)
                if not first:
                    layer_norm(step, n - 1, 0)
                reduce_tiles(step, n, EARLY[0])
                if not first:
                    layer_norm(step, n - 1, 1)
                free_rows(step, [1])
                if not last:
                    reduce_tiles(step, n, EARLY[1])
                    free_rows(step, EARLY[1])
                if not first:
                    invert(step, n - 1, range(2))

            step = Steps()
            make_mask(0)
            classify(step, 0)
            make_perm(step, 0)
            first_head_index(step)
            classify(step, 1)
            first_other_index(step)
            make_perm(step, 1)
            step_of(step, 0, 0, first=True)
            step_of(step, 1, 1)
            step.end()
            with v.Fori(1, B // 2 - 1) as pair:
                step = Steps()
                for side in range(2):
                    step_of(step, 2 * pair + side, side)
                step.end()
            step = Steps()
            step_of(step, B - 2, 0, late=True)
            step_of(step, B - 1, 1, late=True, last=True)
            for g, tiles in enumerate(LAST):
                a, b = tiles[0], tiles[-1] + 1
                reduce_tiles(step, B - 1, [t for t in tiles if t > 2])
                finish_agg(step, B - 1, 1, a, b)
                split_rest(B - 1, a, b, g)
                split_low(B - 1, a, b, g)
            for h in range(2):
                layer_norm(step, B - 1, h)
            for h in range(2):
                invert(step, B - 1, [h])
            v.wait_ge(s_inv, 2 * B)
            v.wait_ge(s_out[1], 16 * (B - 1))
            for t in range(T // 2, T):
                ins = v.tensor_scalar(y[:, t, :], z[:, t, :], inv_std[:, t:t + 1], shift[:, t:t + 1], ALU.mult, ALU.add)
            ins.then_inc(s_y_last, 1)
            step.end()


_INS = ["x", "x_t", "table", "adj_t", "w", "bias", "const"]


def kernel(x, adj, L0_gnn_W, L0_gnn_b):
    import concourse.bacc as _bacc
    from concourse.bass_utils import run_bass_kernel_spmd as _run

    x = np.ascontiguousarray(x)
    arrays = {
        "x": x,
        "x_t": np.ascontiguousarray(x.transpose(0, 2, 1)),
        "table": np.concatenate([np.zeros((B, 1, C), x.dtype), x[:, ::-1]], axis=1).reshape(B * TABLE, C),
        "adj_t": np.ascontiguousarray(np.asarray(adj).transpose(0, 2, 1)),
        "w": np.ascontiguousarray(L0_gnn_W),
        "bias": np.tile(np.asarray(L0_gnn_b).reshape(1, C), (1, 4)),
        "const": constants(),
    }
    nc = _bacc.Bacc("TRN2", target_bir_lowering=False, num_devices=1)
    args = [nc.dram_tensor(f"in_{k}", arrays[k].shape, mybir.dt.from_np(arrays[k].dtype), kind="ExternalInput").ap()
            for k in _INS]
    out = nc.dram_tensor("out_0", (B, N, C), F32, kind="ExternalOutput").ap()
    gnn_kernel(nc, *args, out)
    r = _run(nc, [{f"in_{k}": arrays[k] for k in _INS}], core_ids=[0])
    return r.results[0]["out_0"]
```
